# Optimizing a Trainium2 kernel written in Bass

```python
import numpy as np
import jax
import jax.numpy as jnp

def _softmax(x, axis=-1):
    return jax.nn.softmax(x, axis=axis)

def _gelu(x):
    return jax.nn.gelu(x, approximate=True)

def _silu(x):
    return jax.nn.silu(x)

def _sigmoid(x):
    return jax.nn.sigmoid(x)

def _layernorm(x, axis=-1, eps=1e-05):
    m = jnp.mean(x, axis=axis, keepdims=True)
    v = jnp.var(x, axis=axis, keepdims=True)
    return (x - m) / jnp.sqrt(v + eps)

def _scatter_add(tgt, idx, src, axis=0):
    return tgt.at[idx].add(src)

def _segment_sum(src, seg, n):
    return jax.ops.segment_sum(src, seg, n)
kernel_name = 'mk_xattn_ffn_d2_seqx_r4_a1b745'

def setup_inputs(seed: int=0):
    np.random.seed(seed)
    _w = jnp.asarray

    def _rec_inputs():
        import jax
        import jax.numpy as jnp
        _rk = jax.random.key(seed)
        x = -0.0002928 + 1 * jax.random.normal(jax.random.fold_in(_rk, 1), (8, 256, 256), jnp.float32)
        _lenS = 256 - jax.random.randint(jax.random.fold_in(_rk, 7), (8,), 0, max(1, 256 // 4) + 1, jnp.int32)
        _lenS2 = 256 - jax.random.randint(jax.random.fold_in(_rk, 8), (8,), 0, max(1, 256 // 4) + 1, jnp.int32)
        _ctx_1024P = jax.random.normal(jax.random.fold_in(_rk, 11), (8, 16, 256), jnp.float32)
        _ctx_1024c = jax.random.dirichlet(jax.random.fold_in(_rk, 511), 0.3 * jnp.ones((16,), jnp.float32), (8, 256))
        _ctx_1024t = jnp.einsum('bsk,bkd->bsd', _ctx_1024c, _ctx_1024P)
        _ctx_1024t = _ctx_1024t * jax.lax.rsqrt(jnp.mean(jnp.square(_ctx_1024t)) + 1e-12) * 0.953939
        ctx_1024 = -1.39393e-06 + 0.999914 * (_ctx_1024t + 0.3 * jax.random.normal(jax.random.fold_in(_rk, 611), (8, 256, 256), jnp.float32))
        _validS = jnp.arange(256)[None, :] < _lenS[:, None]
        _validS2 = jnp.arange(256)[None, :] < _lenS2[:, None]
        _causal = jnp.tril(jnp.ones((256, 256), dtype=bool))
        mask_Bx1xSxS2_ik1 = jnp.where(jnp.broadcast_to(_validS2[:, None, None, :], (8, 1, 256, 256)), 1, 0).astype(jnp.int32)
        mask_BxS2_bk0 = jnp.logical_not(jnp.broadcast_to(_validS2[:, :], (8, 256)))
        return (x, ctx_1024, mask_Bx1xSxS2_ik1, mask_BxS2_bk0)
    x, ctx_1024, mask_Bx1xSxS2_ik1, mask_BxS2_bk0 = _rec_inputs()

    def _L0_xattn_setup():
        import jax, jax.numpy as jnp
        import numpy as np
        import math
        D_MODEL = 256
        NUM_HEADS = 16
        D_K = D_MODEL // NUM_HEADS
        B, S = (2, 512)

        def _split_heads(x):
            b, s, _ = x.shape
            return x.reshape(b, s, NUM_HEADS, D_K).transpose(0, 2, 1, 3)
        key = jax.random.key(seed)
        ks = jax.random.split(key, 13)
        scale = 1.0 / math.sqrt(D_MODEL)
        inp = {'q': jax.random.normal(ks[0], (B, S, D_MODEL), jnp.float32), 'k': jax.random.normal(ks[1], (B, S, D_MODEL), jnp.float32), 'v': jax.random.normal(ks[2], (B, S, D_MODEL), jnp.float32), 'mask': jax.random.randint(ks[3], (B, 1, S, S), 0, 2, jnp.int32), 'wQ_w': jax.random.normal(ks[4], (D_MODEL, D_MODEL), jnp.float32) * scale, 'wQ_b': jax.random.normal(ks[5], (D_MODEL,), jnp.float32) * scale, 'wK_w': jax.random.normal(ks[6], (D_MODEL, D_MODEL), jnp.float32) * scale, 'wK_b': jax.random.normal(ks[7], (D_MODEL,), jnp.float32) * scale, 'wV_w': jax.random.normal(ks[8], (D_MODEL, D_MODEL), jnp.float32) * scale, 'wV_b': jax.random.normal(ks[9], (D_MODEL,), jnp.float32) * scale, 'wO_w': jax.random.normal(ks[10], (D_MODEL, D_MODEL), jnp.float32) * scale, 'wO_b': jax.random.normal(ks[11], (D_MODEL,), jnp.float32) * scale}
        return inp
    _L0_xattn_all = _L0_xattn_setup()
    _L0_xattn_in = {k: v for k, v in _L0_xattn_all.items() if k in ('wQ_w', 'wQ_b', 'wK_w', 'wK_b', 'wV_w', 'wV_b', 'wO_w', 'wO_b')}
    del _L0_xattn_all

    def _L0_ffn_setup():
        import jax, jax.numpy as jnp
        import numpy as np
        B, S, D = (2, 512, 256)
        E, K, H = (8, 4, 256)
        SH = 2 * H

        def _silu(x):
            return x * jax.nn.sigmoid(x)

        def _swiglu(x, w1, b1, w2, b2):
            return _silu(x @ w1 + b1) * (x @ w2 + b2)

        def _moe(x, gate_w, exp_w1, exp_w3, exp_w2, sh_w1, sh_w3, sh_w2):
            b, s, d = x.shape
            t = b * s
            xt = x.reshape(t, d)
            scores = jax.nn.softmax(xt @ gate_w.T, axis=-1)
            topv, topi = jax.lax.top_k(scores, K)
            topv = topv / jnp.sum(topv, axis=-1, keepdims=True)
            combine = jnp.zeros((t, E), xt.dtype).at[jnp.arange(t)[:, None], topi].set(topv)
            g = _silu(jnp.einsum('td,edh->eth', xt, exp_w1))
            u = jnp.einsum('td,edh->eth', xt, exp_w3)
            yexp = jnp.einsum('eth,ehd->etd', g * u, exp_w2)
            routed = jnp.einsum('te,etd->td', combine, yexp)
            shared = _silu(xt @ sh_w1) * (xt @ sh_w3) @ sh_w2
            return (routed + shared).reshape(b, s, d)
        key = jax.random.key(seed)
        ks = jax.random.split(key, 24)
        f = lambda k, shape: jax.random.normal(k, shape, dtype=jnp.float32) * 0.02
        return {'x': jax.random.normal(ks[0], (B, S, D), dtype=jnp.float32), 'lin0_w': f(ks[1], (D, D)), 'lin0_b': f(ks[2], (D,)), 'swi1_w1': f(ks[3], (D, D)), 'swi1_b1': f(ks[4], (D,)), 'swi1_w2': f(ks[5], (D, D)), 'swi1_b2': f(ks[6], (D,)), 'gate_w': f(ks[7], (E, D)), 'exp_w1': f(ks[8], (E, D, H)), 'exp_w3': f(ks[9], (E, D, H)), 'exp_w2': f(ks[10], (E, H, D)), 'sh_w1': f(ks[11], (D, SH)), 'sh_w3': f(ks[12], (D, SH)), 'sh_w2': f(ks[13], (SH, D)), 'lin1_w': f(ks[14], (D, D)), 'lin1_b': f(ks[15], (D,)), 'swi2_w1': f(ks[16], (D, D)), 'swi2_b1': f(ks[17], (D,)), 'swi2_w2': f(ks[18], (D, D)), 'swi2_b2': f(ks[19], (D,))}
    _L0_ffn_all = _L0_ffn_setup()
    _L0_ffn_in = {k: v for k, v in _L0_ffn_all.items() if k in ('lin0_w', 'lin0_b', 'swi1_w1', 'swi1_b1', 'swi1_w2', 'swi1_b2', 'gate_w', 'exp_w1', 'exp_w3', 'exp_w2', 'sh_w1', 'sh_w3', 'sh_w2', 'lin1_w', 'lin1_b', 'swi2_w1', 'swi2_b1', 'swi2_w2', 'swi2_b2')}
    del _L0_ffn_all

    def _L1_xattn_setup():
        import jax, jax.numpy as jnp
        import numpy as np
        NUM_HEADS, NUM_KV, HEAD_DIM, WIDTH = (4, 1, 64, 256)
        MASK_FILL = -2.3819763e+38

        def _apply_rope(x, positions, max_wavelength=10000.0):
            d = x.shape[-1]
            freq_exp = 2.0 / d * jnp.arange(d // 2, dtype=jnp.float32)
            timescale = max_wavelength ** freq_exp
            radians = positions[..., None].astype(jnp.float32) / timescale
            radians = radians[..., None, :]
            sin, cos = (jnp.sin(radians), jnp.cos(radians))
            x1, x2 = jnp.split(x, 2, axis=-1)
            out = jnp.concatenate([x1 * cos - x2 * sin, x2 * cos + x1 * sin], axis=-1)
            return out.astype(x.dtype)

        def _rmsnorm(x, scale):
            var = jnp.mean(jnp.square(x.astype(jnp.float32)), axis=-1, keepdims=True)
            normed = x * jax.lax.rsqrt(var + 1e-06)
            return (normed * (1 + scale)).astype(x.dtype)
        key = jax.random.key(seed)
        ks = jax.random.split(key, 7)
        B, T, S = (8, 128, 512)
        return {'x': jax.random.normal(ks[0], (B, T, WIDTH), jnp.float32), 'mem_seq': jax.random.normal(ks[1], (B, S, WIDTH), jnp.float32), 'mem_mask': jax.random.randint(ks[2], (B, S), 0, 2).astype(bool), 'rms_scale': jax.random.normal(ks[3], (WIDTH,), jnp.float32) * 0.02, 'q_w': jax.random.normal(ks[4], (NUM_HEADS, WIDTH, HEAD_DIM), jnp.float32) / np.sqrt(WIDTH), 'kv_w': jax.random.normal(ks[5], (2, NUM_KV, WIDTH, HEAD_DIM), jnp.float32) / np.sqrt(WIDTH), 'out_w': jax.random.normal(ks[6], (NUM_HEADS, HEAD_DIM, WIDTH), jnp.float32) / np.sqrt(NUM_HEADS * HEAD_DIM)}
    _L1_xattn_all = _L1_xattn_setup()
    _L1_xattn_in = {k: v for k, v in _L1_xattn_all.items() if k in ('rms_scale', 'q_w', 'kv_w', 'out_w')}
    del _L1_xattn_all

    def _L1_ffn_setup():
        import jax, jax.numpy as jnp
        import numpy as np
        TOP_K = 2
        key = jax.random.key(seed)
        k0, k1, k2, k3, k4 = jax.random.split(key, 5)
        B, S, H, I, E = (4, 512, 256, 704, 8)
        s_h = 1.0 / np.sqrt(H)
        s_i = 1.0 / np.sqrt(I)
        return {'x': jax.random.normal(k0, (B, S, H), jnp.float32), 'w_router': jax.random.normal(k1, (E, H), jnp.float32) * s_h, 'w_gate': jax.random.normal(k2, (E, I, H), jnp.float32) * s_h, 'w_up': jax.random.normal(k3, (E, I, H), jnp.float32) * s_h, 'w_down': jax.random.normal(k4, (E, H, I), jnp.float32) * s_i}
    _L1_ffn_all = _L1_ffn_setup()
    _L1_ffn_in = {k: v for k, v in _L1_ffn_all.items() if k in ('w_router', 'w_gate', 'w_up', 'w_down')}
    del _L1_ffn_all
    return {'x': x, 'ctx_1024': ctx_1024, 'mask_Bx1xSxS2_ik1': mask_Bx1xSxS2_ik1, 'mask_BxS2_bk0': mask_BxS2_bk0, 'L0_xattn_wQ_w': _L0_xattn_in['wQ_w'], 'L0_xattn_wQ_b': _L0_xattn_in['wQ_b'], 'L0_xattn_wK_w': _L0_xattn_in['wK_w'], 'L0_xattn_wK_b': _L0_xattn_in['wK_b'], 'L0_xattn_wV_w': _L0_xattn_in['wV_w'], 'L0_xattn_wV_b': _L0_xattn_in['wV_b'], 'L0_xattn_wO_w': _L0_xattn_in['wO_w'], 'L0_xattn_wO_b': _L0_xattn_in['wO_b'], 'L0_ffn_lin0_w': _L0_ffn_in['lin0_w'], 'L0_ffn_lin0_b': _L0_ffn_in['lin0_b'], 'L0_ffn_swi1_w1': _L0_ffn_in['swi1_w1'], 'L0_ffn_swi1_b1': _L0_ffn_in['swi1_b1'], 'L0_ffn_swi1_w2': _L0_ffn_in['swi1_w2'], 'L0_ffn_swi1_b2': _L0_ffn_in['swi1_b2'], 'L0_ffn_gate_w': _L0_ffn_in['gate_w'], 'L0_ffn_exp_w1': _L0_ffn_in['exp_w1'], 'L0_ffn_exp_w3': _L0_ffn_in['exp_w3'], 'L0_ffn_exp_w2': _L0_ffn_in['exp_w2'], 'L0_ffn_sh_w1': _L0_ffn_in['sh_w1'], 'L0_ffn_sh_w3': _L0_ffn_in['sh_w3'], 'L0_ffn_sh_w2': _L0_ffn_in['sh_w2'], 'L0_ffn_lin1_w': _L0_ffn_in['lin1_w'], 'L0_ffn_lin1_b': _L0_ffn_in['lin1_b'], 'L0_ffn_swi2_w1': _L0_ffn_in['swi2_w1'], 'L0_ffn_swi2_b1': _L0_ffn_in['swi2_b1'], 'L0_ffn_swi2_w2': _L0_ffn_in['swi2_w2'], 'L0_ffn_swi2_b2': _L0_ffn_in['swi2_b2'], 'L1_xattn_rms_scale': _L1_xattn_in['rms_scale'], 'L1_xattn_q_w': _L1_xattn_in['q_w'], 'L1_xattn_kv_w': _L1_xattn_in['kv_w'], 'L1_xattn_out_w': _L1_xattn_in['out_w'], 'L1_ffn_w_router': _L1_ffn_in['w_router'], 'L1_ffn_w_gate': _L1_ffn_in['w_gate'], 'L1_ffn_w_up': _L1_ffn_in['w_up'], 'L1_ffn_w_down': _L1_ffn_in['w_down']}

def reference(x, ctx_1024, mask_Bx1xSxS2_ik1, mask_BxS2_bk0, L0_xattn_wQ_w, L0_xattn_wQ_b, L0_xattn_wK_w, L0_xattn_wK_b, L0_xattn_wV_w, L0_xattn_wV_b, L0_xattn_wO_w, L0_xattn_wO_b, L0_ffn_lin0_w, L0_ffn_lin0_b, L0_ffn_swi1_w1, L0_ffn_swi1_b1, L0_ffn_swi1_w2, L0_ffn_swi1_b2, L0_ffn_gate_w, L0_ffn_exp_w1, L0_ffn_exp_w3, L0_ffn_exp_w2, L0_ffn_sh_w1, L0_ffn_sh_w3, L0_ffn_sh_w2, L0_ffn_lin1_w, L0_ffn_lin1_b, L0_ffn_swi2_w1, L0_ffn_swi2_b1, L0_ffn_swi2_w2, L0_ffn_swi2_b2, L1_xattn_rms_scale, L1_xattn_q_w, L1_xattn_kv_w, L1_xattn_out_w, L1_ffn_w_router, L1_ffn_w_gate, L1_ffn_w_up, L1_ffn_w_down):
    import jax
    import jax.numpy as jnp

    def _L0_xattn_ref(q, k, v, mask, wQ_w, wQ_b, wK_w, wK_b, wV_w, wV_b, wO_w, wO_b):
        import jax, jax.numpy as jnp
        import numpy as np
        import math
        D_MODEL = 256
        NUM_HEADS = 16
        D_K = D_MODEL // NUM_HEADS
        B, S = (2, 512)

        def _split_heads(x):
            b, s, _ = x.shape
            return x.reshape(b, s, NUM_HEADS, D_K).transpose(0, 2, 1, 3)
        qh = _split_heads(q @ wQ_w.T + wQ_b)
        kh = _split_heads(k @ wK_w.T + wK_b)
        vh = _split_heads(v @ wV_w.T + wV_b)
        scores = jnp.einsum('bhsd,bhtd->bhst', qh, kh) / math.sqrt(D_K)
        scores = jnp.where(mask == 0, jnp.float32(-1000000000.0), scores)
        attn = jax.nn.softmax(scores, axis=-1)
        out = jnp.einsum('bhst,bhtd->bhsd', attn, vh)
        out = out.transpose(0, 2, 1, 3).reshape(q.shape[0], -1, D_MODEL)
        return out @ wO_w.T + wO_b

    def _L0_ffn_ref(x, lin0_w, lin0_b, swi1_w1, swi1_b1, swi1_w2, swi1_b2, gate_w, exp_w1, exp_w3, exp_w2, sh_w1, sh_w3, sh_w2, lin1_w, lin1_b, swi2_w1, swi2_b1, swi2_w2, swi2_b2):
        import jax, jax.numpy as jnp
        import numpy as np
        B, S, D = (2, 512, 256)
        E, K, H = (8, 4, 256)
        SH = 2 * H

        def _silu(x):
            return x * jax.nn.sigmoid(x)

        def _swiglu(x, w1, b1, w2, b2):
            return _silu(x @ w1 + b1) * (x @ w2 + b2)

        def _moe(x, gate_w, exp_w1, exp_w3, exp_w2, sh_w1, sh_w3, sh_w2):
            b, s, d = x.shape
            t = b * s
            xt = x.reshape(t, d)
            scores = jax.nn.softmax(xt @ gate_w.T, axis=-1)
            topv, topi = jax.lax.top_k(scores, K)
            topv = topv / jnp.sum(topv, axis=-1, keepdims=True)
            combine = jnp.zeros((t, E), xt.dtype).at[jnp.arange(t)[:, None], topi].set(topv)
            g = _silu(jnp.einsum('td,edh->eth', xt, exp_w1))
            u = jnp.einsum('td,edh->eth', xt, exp_w3)
            yexp = jnp.einsum('eth,ehd->etd', g * u, exp_w2)
            routed = jnp.einsum('te,etd->td', combine, yexp)
            shared = _silu(xt @ sh_w1) * (xt @ sh_w3) @ sh_w2
            return (routed + shared).reshape(b, s, d)
        h = x @ lin0_w + lin0_b
        h = _swiglu(h, swi1_w1, swi1_b1, swi1_w2, swi1_b2)
        h = _moe(h, gate_w, exp_w1, exp_w3, exp_w2, sh_w1, sh_w3, sh_w2)
        h = h @ lin1_w + lin1_b
        h = _swiglu(h, swi2_w1, swi2_b1, swi2_w2, swi2_b2)
        return h

    def _L1_xattn_ref(x, mem_seq, mem_mask, rms_scale, q_w, kv_w, out_w):
        import jax, jax.numpy as jnp
        import numpy as np
        NUM_HEADS, NUM_KV, HEAD_DIM, WIDTH = (4, 1, 64, 256)
        MASK_FILL = -2.3819763e+38

        def _apply_rope(x, positions, max_wavelength=10000.0):
            d = x.shape[-1]
            freq_exp = 2.0 / d * jnp.arange(d // 2, dtype=jnp.float32)
            timescale = max_wavelength ** freq_exp
            radians = positions[..., None].astype(jnp.float32) / timescale
            radians = radians[..., None, :]
            sin, cos = (jnp.sin(radians), jnp.cos(radians))
            x1, x2 = jnp.split(x, 2, axis=-1)
            out = jnp.concatenate([x1 * cos - x2 * sin, x2 * cos + x1 * sin], axis=-1)
            return out.astype(x.dtype)

        def _rmsnorm(x, scale):
            var = jnp.mean(jnp.square(x.astype(jnp.float32)), axis=-1, keepdims=True)
            normed = x * jax.lax.rsqrt(var + 1e-06)
            return (normed * (1 + scale)).astype(x.dtype)
        B, S, _ = mem_seq.shape
        T = x.shape[1]
        G = NUM_HEADS // NUM_KV
        xn = _rmsnorm(x, rms_scale)
        mn = _rmsnorm(mem_seq, rms_scale)
        q = jnp.einsum('BTD,NDH->BTNH', xn, q_w)
        kv = jnp.einsum('BSD,cKDH->cBSKH', mn, kv_w)
        k, v = (kv[0], kv[1])
        q_pos = jnp.broadcast_to(jnp.arange(S, T + S), (B, T))
        k_pos = jnp.broadcast_to(jnp.arange(S), (B, S))
        q = _apply_rope(q, q_pos) * HEAD_DIM ** (-0.5)
        k = _apply_rope(k, k_pos)
        q = q.reshape(B, T, NUM_KV, G, HEAD_DIM)
        logits = jnp.einsum('BTKGH,BSKH->BKGTS', q, k, preferred_element_type=jnp.float32)
        masked = jnp.where(mem_mask[:, None, None, None, :], logits, MASK_FILL)
        probs = jax.nn.softmax(masked, axis=-1).astype(x.dtype)
        enc = jnp.einsum('BKGTS,BSKH->BTKGH', probs, v).reshape(B, T, NUM_HEADS, HEAD_DIM)
        return jnp.einsum('BTNH,NHD->BTD', enc, out_w)

    def _L1_ffn_ref(x, w_router, w_gate, w_up, w_down):
        import jax, jax.numpy as jnp
        import numpy as np
        TOP_K = 2
        B, S, H = x.shape
        E = w_router.shape[0]
        xf = x.reshape(-1, H)
        logits = jnp.einsum('th,eh->te', xf, w_router)
        probs = jax.nn.softmax(logits, axis=-1)
        topw, topi = jax.lax.top_k(probs, TOP_K)
        topw = topw / jnp.sum(topw, axis=-1, keepdims=True)
        onehot = (topi[..., None] == jnp.arange(E)).astype(x.dtype)
        combine = jnp.einsum('tk,tke->te', topw, onehot)
        gate = jax.nn.silu(jnp.einsum('th,eih->eti', xf, w_gate))
        up = jnp.einsum('th,eih->eti', xf, w_up)
        down = jnp.einsum('eti,ehi->eth', gate * up, w_down)
        out = jnp.einsum('eth,te->th', down, combine)
        return out.reshape(B, S, H)
    x = x + _L0_xattn_ref(_layernorm(x, axis=-1), ctx_1024, ctx_1024, mask_Bx1xSxS2_ik1, L0_xattn_wQ_w, L0_xattn_wQ_b, L0_xattn_wK_w, L0_xattn_wK_b, L0_xattn_wV_w, L0_xattn_wV_b, L0_xattn_wO_w, L0_xattn_wO_b)
    x = x + _L0_ffn_ref(_layernorm(x, axis=-1), L0_ffn_lin0_w, L0_ffn_lin0_b, L0_ffn_swi1_w1, L0_ffn_swi1_b1, L0_ffn_swi1_w2, L0_ffn_swi1_b2, L0_ffn_gate_w, L0_ffn_exp_w1, L0_ffn_exp_w3, L0_ffn_exp_w2, L0_ffn_sh_w1, L0_ffn_sh_w3, L0_ffn_sh_w2, L0_ffn_lin1_w, L0_ffn_lin1_b, L0_ffn_swi2_w1, L0_ffn_swi2_b1, L0_ffn_swi2_w2, L0_ffn_swi2_b2)
    x = x + _L1_xattn_ref(_layernorm(x, axis=-1), ctx_1024, mask_BxS2_bk0, L1_xattn_rms_scale, L1_xattn_q_w, L1_xattn_kv_w, L1_xattn_out_w)
    x = x + _L1_ffn_ref(_layernorm(x, axis=-1), L1_ffn_w_router, L1_ffn_w_gate, L1_ffn_w_up, L1_ffn_w_down)
    return x

_drawn_inputs = setup_inputs


def setup_inputs(seed=0):
    import zlib

    import numpy as np

    out = dict(_drawn_inputs(seed))
    spreads = {}
    factors = {}
    for name, (base, spread) in spreads.items():
        noise = np.random.default_rng([zlib.crc32(name.encode()), seed]).standard_normal(out[name].shape)
        drawn = base * np.exp(spread * noise) if base else spread * noise
        out[name] = jnp.asarray(drawn.astype(out[name].dtype))
    for name, factor in factors.items():
        out[name] = (out[name] * factor).astype(out[name].dtype)
    return out
```

```python
import concourse.bass as bass
from concourse import mybir
from contextlib import ExitStack

F32 = mybir.dt.float32
F32R = mybir.dt.float32r
I32 = mybir.dt.int32
U8 = mybir.dt.uint8
U32 = mybir.dt.uint32
ACT = mybir.ActivationFunctionType
ALU = mybir.AluOpType
AX = mybir.AxisListType

B, S, D = 8, 256, 256
P = 128
KC = D // P
TOK = B * S
NT = TOK // P
ST = S // P
CH = 512
NCH = TOK // CH
TPC = CH // P
LN_EPS = 1e-5
HEADS, HD = 16, 16
MASKED = float(2 ** 30)


def split_products(pe, out, stationary, moving, first, last):
    (sh, sl), (mh, ml) = stationary, moving
    pe.matmul(out, sh, mh, start=first, stop=False)
    pe.matmul(out, sh, ml, start=False, stop=False)
    return pe.matmul(out, sl, mh, start=False, stop=last)


def held(eng, t):
    eng.sem_inc(t["passed"], 1)


def f32(ap):
    return ap.bitcast(F32)


def project_columns(pe, out, w, x):
    for m in range(KC):
        for kc in range(KC):
            last = split_products(pe, out[:, m, :],
                                  (w[0][:, kc, bass.ts(m, P)], w[1][:, kc, bass.ts(m, P)]),
                                  (x[0][:, kc, :], x[1][:, kc, :]), kc == 0, kc == KC - 1)
    return last


def attention0_projections(nc, sem, t, a):
    with ExitStack() as ctx:
        def tile(name, shape, dt=F32):
            return ctx.enter_context(nc.sbuf_tensor(name, shape, dt))

        def bank(name, shape):
            return ctx.enter_context(nc.psum_tensor(name, shape, F32))

        chunks = 2 * NCH
        w_raw = tile("w_raw", [P, 3, KC, D])
        w_hi = tile("w_hi", [P, 3, KC, D], F32R)
        w_lo = tile("w_lo", [P, 3, KC, D], F32R)
        rows = tile("rows", [P, 2, TPC, D])
        chunk_hi = tile("chunk_hi", [P, 2, KC, CH], F32R)
        chunk_lo = tile("chunk_lo", [P, 2, KC, CH], F32R)
        qk_bias = tile("qk_bias", [P, 2, KC])
        v_bias = tile("v_bias", [P, D])
        mask_raw = tile("mask_raw", [P, NT, S], I32)
        stats = tile("stats", [P, NT, 6])
        mean_var = tile("mean_var", [P, NT, 2])
        std = tile("std", [P, NT])
        rstd = tile("rstd", [P, NT])
        turned = bank("turned", [P, KC, CH])
        projected = bank("projected", [P, 2, KC, CH])
        v_rows = projected[:, 1].rearrange("p k n -> p (k n)").rearrange("p (j d) -> p j d", j=TPC)

        loaded_w = [sem(f"p1_loaded_w{n}") for n in range(4)]
        loaded_ctx = [sem(f"p1_loaded_ctx{n}") for n in range(2)]
        names = ("loaded_ident loaded_x loaded_small loaded_mask split_w split_wo eps_set ident_rounded turned_ready "
                 "split_hi split_lo k_ready v_ready k_hi k_lo v_out stats_step stats_done std_done rstd_done normed "
                 "q_ready q_hi q_lo masked_found valid_found scaled").split()
        s = {n: sem("p1_" + n) for n in names}
        masked = t["mask_bias"]

        block = ctx.enter_context(nc.Block())

        @block.sync
        def _(sp):
            sp.dma_start(t["ident"][:], a["ident"]).then_inc(s["loaded_ident"], 16)
            for c in range(NCH):
                if c >= 2:
                    sp.wait_ge(s["turned_ready"], c - 1)
                sp.dma_start(rows[:, c % 2], a["ctx"][c * CH:(c + 1) * CH, :].rearrange("(j p) d -> p j d", p=P))\
                    .then_inc(loaded_ctx[c % 2], 16)
                if c == 1:
                    sp.dma_start(t["head_rows"][:], a["head_rows"]).then_inc(s["loaded_small"], 16)
                    for n, name in enumerate(("bQ", "bK")):
                        sp.dma_start(qk_bias[:, n, :], a[name]).then_inc(s["loaded_small"], 16)
                    for dst, name in ((v_bias, "bV"), (t["o_bias"], "bO")):
                        sp.dma_start(dst[:], a[name].partition_broadcast(P)).then_inc(s["loaded_small"], 16)

        @block.scalar
        def _(act):
            for n, name in enumerate(("wK", "wV", "wQ")):
                act.dma_start(w_raw[:, n], a[name].rearrange("(k p) n -> p k n", p=P)).then_inc(loaded_w[n], 16)
            act.dma_start(t["x_res"][:], a["x"].rearrange("(j p) d -> p j d", p=P)).then_inc(s["loaded_x"], 16)
            act.dma_start(t["wo_raw"][:], a["wO"].rearrange("(k p) n -> p k n", p=P)).then_inc(loaded_w[3], 16)
            act.dma_start(mask_raw[:], a["mask0"].rearrange("(j p) k -> p j k", p=P)).then_inc(s["loaded_mask"], 16)

            def high_parts(c):
                act.wait_ge(s["turned_ready"], c + 1)
                if c >= 2:
                    act.wait_ge(s["k_ready"], min(c - 1, NCH))
                    act.wait_ge(s["v_ready"], min(c - 1, NCH))
                if c - 2 >= NCH:
                    act.wait_ge(s["q_ready"], c - 1 - NCH)
                act.activation(chunk_hi[:, c % 2], turned[:], ACT.Copy).then_inc(s["split_hi"], 1)

            high_parts(0)
            act.wait_ge(s["loaded_ident"], 16)
            act.activation(t["ident_r"][:], t["ident"][:], ACT.Copy).then_inc(s["ident_rounded"], 1)
            act.wait_ge(s["loaded_small"], 80)
            for c in range(chunks):
                if c + 1 < chunks:
                    high_parts(c + 1)
                if c == 2:
                    act.wait_ge(s["eps_set"], 1)
                    act.wait_ge(s["stats_done"], NT)
                    act.activation(std[:], mean_var[:, :, 1], ACT.Sqrt, bias=t["ln_eps"][:])\
                        .then_inc(s["std_done"], 1)
                n, n_bias, dst, ready, done = (c, 1, "kT_hi", "k_ready", "k_hi") if c < NCH else \
                    (c - NCH, 0, "qT_hi", "q_ready", "q_hi")
                act.wait_ge(s[ready], n + 1)
                out = projected[:, 0 if c < NCH else n % 2]
                for m in range(KC):
                    act.activation(t[dst][:, m, bass.ts(n, CH)], out[:, m, :], ACT.Identity,
                                   bias=qk_bias[:, n_bias, m:m + 1]).then_inc(s[done], 1)

        @block.gpsimd
        def _(pool):
            pool.memset(t["ln_eps"][:], LN_EPS).then_inc(s["eps_set"], 1)
            for n in range(3):
                pool.wait_ge(loaded_w[n], 16)
                pool.tensor_copy(w_hi[:, n], w_raw[:, n]).then_inc(s["split_w"], 1)
                pool.wait_ge(s["split_w"], 2 * n + 1)
                pool.tensor_tensor(w_lo[:, n], w_raw[:, n], f32(w_hi[:, n]), ALU.subtract).then_inc(s["split_w"], 1)
            pool.wait_ge(s["loaded_mask"], 16)
            pool.tensor_scalar(masked[:], mask_raw[:], 0, None, ALU.is_equal).then_inc(s["masked_found"], 1)
            pool.wait_ge(loaded_w[3], 16)
            pool.tensor_copy(t["wo_hi"][:], t["wo_raw"][:]).then_inc(s["split_wo"], 1)
            pool.wait_ge(s["split_wo"], 1)
            pool.tensor_tensor(t["wo_lo"][:], t["wo_raw"][:], f32(t["wo_hi"][:]), ALU.subtract)\
                .then_inc(s["split_wo"], 1)
            pool.wait_ge(s["valid_found"], 1)
            for name, factor in (("scale", -HD ** -0.5), ("neg_scale", HD ** -0.5), ("mask_depth", MASKED)):
                pool.tensor_scalar(t[name][:], t["all_masked"][:], -1.0, factor, ALU.add, ALU.mult)\
                    .then_inc(s["scaled"], 1)
            pool.wait_ge(s["scaled"], 3)
            pool.tensor_tensor(masked[:], f32(masked[:]), t["mask_depth"][:].unsqueeze(2).to_broadcast([P, NT, S]),
                               ALU.mult).then_inc(s["scaled"], 1)

        @block.vector
        def _(dve):
            def low_parts(c):
                dve.wait_ge(s["split_hi"], c + 1)
                dve.tensor_tensor(chunk_lo[:, c % 2], turned[:], f32(chunk_hi[:, c % 2]), ALU.subtract)\
                    .then_inc(s["split_lo"], 1)

            low_parts(0)
            dve.wait_ge(s["loaded_small"], 80)
            for c in range(chunks):
                if c + 1 < chunks:
                    low_parts(c + 1)
                if c == 2:
                    dve.wait_ge(s["std_done"], 1)
                    dve.reciprocal(rstd[:], std[:]).then_inc(s["rstd_done"], 1)
                    dve.wait_ge(s["rstd_done"], 1)
                if NCH <= c + 2 < chunks:
                    dve.wait_ge(s["turned_ready"], c + 1)
                    for j in range(TPC):
                        n = (c + 2 - NCH) * TPC + j
                        last = dve.tensor_scalar(rows[:, c % 2, j, :], t["x_res"][:, n, :], mean_var[:, n, 0:1],
                                                 rstd[:, n:n + 1], ALU.subtract, ALU.mult)
                    last.then_inc(s["normed"], 1)
                n, n_bias, dst, hi, lo = (c, 1, "kT", "k_hi", "k_lo") if c < NCH else (c - NCH, 0, "qT", "q_hi", "q_lo")
                out = projected[:, 0 if c < NCH else n % 2]
                for m in range(KC):
                    dve.wait_ge(s[hi], n * KC + m + 1)
                    dve.scalar_tensor_tensor(t[dst + "_lo"][:, m, bass.ts(n, CH)], out[:, m, :],
                                             qk_bias[:, n_bias, m:m + 1], f32(t[dst + "_hi"][:, m, bass.ts(n, CH)]),
                                             ALU.add, ALU.subtract).then_inc(s[lo], 1)
                if c < NCH:
                    dve.wait_ge(s["v_ready"], c + 1)
                    dve.tensor_tensor(t["v_all"][:, c * TPC:(c + 1) * TPC, :], v_rows,
                                      v_bias[:].unsqueeze(1).to_broadcast([P, TPC, D]), ALU.add)\
                        .then_inc(s["v_out"], 1)
                if c == 0:
                    dve.wait_ge(s["loaded_x"], 16)
                    for j in range(NT):
                        dve.bn_stats(stats[:, j, :], t["x_res"][:, j, :]).then_inc(s["stats_step"], 1)
                if c == 1:
                    for j in range(NT):
                        dve.wait_ge(s["stats_step"], j + 1)
                        dve.bn_aggr(mean_var[:, j, :], stats[:, j, :]).then_inc(s["stats_done"], 1)
                if c == 2:
                    dve.wait_ge(s["masked_found"], 1)
                    dve.tensor_reduce(t["all_masked"][:], f32(masked[:]), AX.X, ALU.min)\
                        .then_inc(s["valid_found"], 1)

        @block.tensor
        def _(pe):
            def turn_rows(c):
                if c < NCH:
                    pe.wait_ge(loaded_ctx[c % 2], 16 * (c // 2 + 1))
                else:
                    pe.wait_ge(s["normed"], c - NCH + 1)
                if c >= 1:
                    pe.wait_ge(s["split_lo"], c)
                for kc in range(KC):
                    for j in range(TPC):
                        last = pe.transpose(turned[:, kc, bass.ts(j, P)], rows[:, c % 2, j, bass.ts(kc, P)],
                                            t["ident"][:])
                last.then_inc(s["turned_ready"], 1)

            def project(n, c, out):
                return project_columns(pe, out, (w_hi[:, n], w_lo[:, n]), (chunk_hi[:, c % 2], chunk_lo[:, c % 2]))

            pe.wait_ge(s["loaded_ident"], 16)
            turn_rows(0)
            for c in range(chunks):
                if c + 1 < chunks:
                    turn_rows(c + 1)
                pe.wait_ge(s["split_lo"], c + 1)
                if c < NCH:
                    pe.wait_ge(s["split_w"], 2)
                    if c >= 1:
                        pe.wait_ge(s["k_lo"], c * KC)
                    project(0, c, projected[:, 0]).then_inc(s["k_ready"], 1)
                    pe.wait_ge(s["split_w"], 4)
                    if c >= 1:
                        pe.wait_ge(s["v_out"], c)
                    for j in range(TPC):
                        for kc in range(KC):
                            last = split_products(
                                pe, v_rows[:, j, :],
                                (chunk_hi[:, c % 2, kc, bass.ts(j, P)], chunk_lo[:, c % 2, kc, bass.ts(j, P)]),
                                (w_hi[:, 1, kc, :], w_lo[:, 1, kc, :]), kc == 0, kc == KC - 1)
                    last.then_inc(s["v_ready"], 1)
                else:
                    n = c - NCH
                    pe.wait_ge(s["split_w"], 6)
                    pe.wait_ge(s["k_lo"], NCH * KC)
                    pe.wait_ge(s["v_out"], NCH)
                    if n >= 2:
                        pe.wait_ge(s["q_lo"], (n - 1) * KC)
                    project(2, c, projected[:, n % 2]).then_inc(s["q_ready"], 1)


HG = 4
NG = HEADS // HG
S_RING = 4
W_RING = 4


def attention0(nc, sem, t, a):
    with ExitStack() as ctx:
        def tile(name, shape, dt=F32):
            return ctx.enter_context(nc.sbuf_tensor(name, shape, dt))

        def bank(name, shape):
            return ctx.enter_context(nc.psum_tensor(name, shape, F32))

        q_hi = tile("qh_hi", [P, HEADS, S], F32R)
        q_lo = tile("qh_lo", [P, HEADS, S], F32R)
        peak = tile("peak", [P, S_RING, ST])
        shift = tile("shift", [P, S_RING, ST])
        weights = tile("weights", [P, W_RING, ST, S])
        weightsT = tile("weightsT", [P, 2 * HG, ST, S])
        v_aug = tile("v_aug", [P, ST, HEADS, 2 * HD])
        outT = tile("outT", [P, NG, S])
        total_inv = tile("total_inv", [P, HEADS])
        out_rows = tile("out_rows", [P, ST, D])
        oT_hi = tile("oT_hi", [P, KC, S], F32R)
        oT_lo = tile("oT_lo", [P, KC, S], F32R)
        scores = bank("scores", [P, S_RING, ST * S])
        wT = bank("wT", [P, 2, ST, S])
        values = bank("values", [P, 2, S])
        tail = bank("tail", [P, CH])

        q_masked = sem("a0_q_masked")
        ones_set = sem("a0_ones_set")
        v_copied = sem("a0_v_copied")
        s_ready = sem("a0_s_ready")
        peak_found = sem("a0_peak_found")
        shift_ready = sem("a0_shift_ready")
        w_ready = sem("a0_w_ready")
        w_turned = sem("a0_w_turned")
        wT_dve = sem("a0_wT_dve")
        wT_act = sem("a0_wT_act")
        pv_ready = sem("a0_pv_ready")
        outT_ready = sem("a0_outT_ready")
        out_turned = sem("a0_out_turned")
        total_ready = sem("a0_total_ready")
        out_normed = sem("a0_out_normed")
        oT_ready = sem("a0_oT_ready")
        oT_hi_ready = sem("a0_oT_hi_ready")
        oT_lo_ready = sem("a0_oT_lo_ready")
        o_ready = sem("a0_o_ready")
        res_added = sem("a0_res_added")
        residual_biased = sem("a0_residual_biased")

        block = ctx.enter_context(nc.Block())

        def each_batch(eng, body):
            body(0, True, False)
            with eng.Fori(1, B) as b:
                body(b, False, False)
            body(B, False, True)

        def copied(eng, b, h):
            g, r = divmod(h, HG)
            if r == HG - 1:
                eng.wait_ge(wT_act, b * NG + (g + 1))
            else:
                eng.wait_ge(wT_dve, b * (HEADS - NG) + (g * (HG - 1) + r + 1))

        @block.gpsimd
        def _(pool):
            def masked_q(b, g, first):
                kc, h0 = divmod(g * HG, P // HD)
                if not first:
                    pool.wait_ge(s_ready, (b - 1) * HEADS + (g + 1) * HG)
                held(pool, t)
                for src, dst in (("qT_hi", q_hi), ("qT_lo", q_lo)):
                    last = pool.tensor_tensor(
                        dst[:, g * HG:(g + 1) * HG, :],
                        f32(t[src][:, kc, bass.ts(b, S)]).unsqueeze(1).to_broadcast([P, HG, S]),
                        t["head_rows"][:, h0:h0 + HG].unsqueeze(2).to_broadcast([P, HG, S]), ALU.mult)
                last.then_inc(q_masked, 1)

            def batch_values(b, first):
                if not first:
                    pool.wait_ge(pv_ready, b * NG)
                held(pool, t)
                pool.tensor_copy(v_aug[:, :, :, 0:HD],
                                 t["v_all"][:, bass.ds(b * ST, ST), :].rearrange("p k (h c) -> p k h c", c=HD))\
                    .then_inc(v_copied, 1)

            pool.memset(v_aug[:], 1.0).then_inc(ones_set, 1)
            for g in range(NG):
                masked_q(0, g, True)
            pool.wait_ge(ones_set, 1)
            batch_values(0, True)
            pool.tensor_tensor(t["x_res"][:], t["x_res"][:],
                               t["o_bias"][:].unsqueeze(1).to_broadcast([P, NT, D]), ALU.add)\
                .then_inc(residual_biased, 1)
            with pool.Fori(1, B) as b:
                for g in range(NG):
                    masked_q(b, g, False)
                batch_values(b, False)

        @block.vector
        def _(dve):
            def peaks(b, h):
                dve.wait_ge(s_ready, b * HEADS + (h + 1))
                r = h % S_RING
                dve.tensor_reduce(peak[:, r, :], scores[:, r, :].rearrange("p (q k) -> p q k", q=ST),
                                  AX.X, ALU.max).then_inc(peak_found, 1)
                dve.wait_ge(peak_found, b * HEADS + (h + 1))
                dve.tensor_tensor(shift[:, r, :], peak[:, r, :], t["neg_scale"][:, bass.ds(b * ST, ST)],
                                  ALU.mult).then_inc(shift_ready, 1)

            def copy_wT(b, h, first):
                g = h // HG
                if h % HG == HG - 1:
                    return
                dve.wait_ge(w_turned, b * HEADS + (h + 1))
                if not (first and g < 2):
                    dve.wait_ge(pv_ready, b * NG + (g - 1))
                dve.tensor_copy(weightsT[:, h % (2 * HG)], wT[:, h % 2]).then_inc(wT_dve, 1)

            def normalise(b, q):
                dve.wait_ge(out_turned, b * ST + (q + 1))
                heads = tail[:].rearrange("p (h c) -> p h c", c=2 * HD)
                dve.reciprocal(total_inv[:], heads[:, :, HD]).then_inc(total_ready, 1)
                dve.wait_ge(total_ready, b * ST + (q + 1))
                dve.tensor_tensor(out_rows[:, q, :].rearrange("p (h c) -> p h c", c=HD), heads[:, :, 0:HD],
                                  total_inv[:].unsqueeze(2).to_broadcast([P, HEADS, HD]), ALU.mult)\
                    .then_inc(out_normed, 1)

            def body(b, first, tail_only):
                for h in range(HEADS):
                    if tail_only and h > 10:
                        break
                    if not tail_only:
                        peaks(b, h)
                    if h >= 2 and not tail_only:
                        copy_wT(b, h - 2, first)
                    if first:
                        continue
                    if h < 2:
                        copy_wT(b - 1, HEADS - 2 + h, False)
                    if h in (5, 6):
                        normalise(b - 1, h - 5)
                    if h == 8:
                        dve.wait_ge(oT_hi_ready, b)
                        dve.tensor_tensor(oT_lo[:], tail[:].rearrange("p (k q) -> p k q", k=KC), f32(oT_hi[:]),
                                          ALU.subtract).then_inc(oT_lo_ready, 1)
                    if h == 10:
                        dve.wait_ge(o_ready, b)
                        dve.wait_ge(residual_biased, 1)
                        dve.tensor_tensor(t["x_res"][:, bass.ds((b - 1) * ST, ST), :],
                                          tail[:].rearrange("p (q d) -> p q d", q=ST),
                                          t["x_res"][:, bass.ds((b - 1) * ST, ST), :], ALU.add)\
                            .then_inc(res_added, 1)

            dve.sem_inc(res_added, 1)
            each_batch(dve, body)

        @block.scalar
        def _(act):
            def softmax_weights(b, h, first):
                r = h % S_RING
                act.wait_ge(shift_ready, b * HEADS + (h + 1))
                if not (first and h < W_RING):
                    act.wait_ge(w_turned, b * HEADS + (h - W_RING + 1))
                held(act, t)
                for q in range(ST):
                    last = act.activation(weights[:, r, q, :], scores[:, r, bass.ts(q, S)], ACT.Exp,
                                          bias=shift[:, r, q:q + 1],
                                          scale=t["scale"][:, bass.ds(b * ST + q, 1)])
                last.then_inc(w_ready, 1)

            def copy_wT(b, h, first):
                if h % HG != HG - 1:
                    return
                act.wait_ge(w_turned, b * HEADS + (h + 1))
                if not (first and h // HG < 2):
                    act.wait_ge(pv_ready, b * NG + (h // HG - 1))
                act.activation(weightsT[:, h % (2 * HG)], wT[:, h % 2], ACT.Copy).then_inc(wT_act, 1)

            def copy_outT(b, pair, first):
                act.wait_ge(pv_ready, b * NG + 2 * (pair + 1))
                if not first:
                    act.wait_ge(out_turned, b * ST)
                act.activation(outT[:, 2 * pair:2 * pair + 2], values[:], ACT.Copy).then_inc(outT_ready, 1)

            def body(b, first, tail_only):
                for h in range(HEADS):
                    if tail_only and h > 10:
                        break
                    if not tail_only:
                        softmax_weights(b, h, first)
                    if h >= 2 and not tail_only:
                        copy_wT(b, h - 2, first)
                    if h == 12 and not tail_only:
                        copy_outT(b, 0, first)
                    if first:
                        continue
                    if h < 2:
                        copy_wT(b - 1, HEADS - 2 + h, False)
                    if h == 4:
                        copy_outT(b - 1, 1, True)
                    if h == 8:
                        act.wait_ge(oT_ready, b)
                        act.activation(oT_hi[:], tail[:].rearrange("p (k q) -> p k q", k=KC), ACT.Copy)\
                            .then_inc(oT_hi_ready, 1)

            each_batch(act, body)

        @block.tensor
        def _(pe):
            def head_scores(b, h, first):
                r, kc = h % S_RING, h * HD // P
                if h % HG == 0:
                    pe.wait_ge(q_masked, b * NG + (h // HG + 1))
                if not (first and h < S_RING):
                    pe.wait_ge(w_ready, b * HEADS + (h - S_RING + 1))
                for q in range(ST):
                    out = scores[:, r, bass.ts(q, S)]
                    pe.matmul(out, t["ident_r"][:],
                              t["mask_bias"][:, bass.ds(b * ST + q, 1), :].rearrange("p o k -> p (o k)"),
                              start=True, stop=False)
                    last = split_products(
                        pe, out, (q_hi[:, h, bass.ts(q, P)], q_lo[:, h, bass.ts(q, P)]),
                        (t["kT_hi"][:, kc, bass.ts(b, S)], t["kT_lo"][:, kc, bass.ts(b, S)]), False, True)
                last.then_inc(s_ready, 1)

            def turn_weights(b, h, first):
                pe.wait_ge(w_ready, b * HEADS + (h + 1))
                if not (first and h < 2):
                    copied(pe, b if h >= 2 else b - 1, (h - 2) % HEADS)
                for k in range(ST):
                    for q in range(ST):
                        last = pe.transpose(wT[:, h % 2, k, bass.ts(q, P)], weights[:, h % W_RING, q, bass.ts(k, P)],
                                            t["ident"][:])
                last.then_inc(w_turned, 1)

            def group_values(b, g, first):
                copied(pe, b, g * HG + HG - 2)
                copied(pe, b, g * HG + HG - 1)
                if not (first and g < 2) and g % 2 == 0:
                    pe.wait_ge(outT_ready, b * 2 + g // 2)
                if g == 0:
                    pe.wait_ge(v_copied, b + 1)
                for k in range(ST):
                    for r in range(HG):
                        h = g * HG + r
                        last = pe.matmul(values[32 * r:32 * r + 32, g % 2, :], v_aug[:, k, h, :],
                                         weightsT[:, h % (2 * HG), k, :], start=(k == 0), stop=(k == ST - 1))
                last.then_inc(pv_ready, 1)

            def body(b, first, tail_only):
                for h in range(HEADS):
                    if tail_only and h > 10:
                        break
                    if not tail_only:
                        head_scores(b, h, first)
                        if h >= 2:
                            turn_weights(b, h - 2, first)
                        if h in (7, 11, 15):
                            group_values(b, (h - 7) // HG, first)
                    if first:
                        continue
                    if h < 2:
                        turn_weights(b - 1, HEADS - 2 + h, False)
                    if h == 3:
                        group_values(b - 1, NG - 1, False)
                    if h in (5, 6):
                        q = h - 5
                        pe.wait_ge(outT_ready, 2 * b)
                        if q == 0:
                            pe.wait_ge(res_added, b)
                        else:
                            pe.wait_ge(out_normed, (b - 1) * ST + 1)
                        for g in range(NG):
                            last = pe.transpose(tail[:, bass.ts(g, P)], outT[:, g, bass.ts(q, P)], t["ident"][:])
                        last.then_inc(out_turned, 1)
                    if h == 8:
                        pe.wait_ge(out_normed, b * ST)
                        for k in range(KC):
                            for q in range(ST):
                                last = pe.transpose(tail[:, k * S + q * P:k * S + (q + 1) * P],
                                                    out_rows[:, q, bass.ts(k, P)], t["ident"][:])
                        last.then_inc(oT_ready, 1)
                    if h == 10:
                        pe.wait_ge(oT_lo_ready, b)
                        for q in range(ST):
                            for kc in range(KC):
                                last = split_products(
                                    pe, tail[:, bass.ts(q, D)],
                                    (oT_hi[:, kc, bass.ts(q, P)], oT_lo[:, kc, bass.ts(q, P)]),
                                    (t["wo_hi"][:, kc, :], t["wo_lo"][:, kc, :]), kc == 0, kc == KC - 1)
                        last.then_inc(o_ready, 1)

            each_batch(pe, body)


EXPERTS = 8
HALVES = EXPERTS + 2


def split_weights(pool, raw, hi, lo, done, count):
    pool.tensor_copy(hi, raw).then_inc(done, 1)
    pool.wait_ge(done, count + 1)
    pool.tensor_tensor(lo, raw, f32(hi), ALU.subtract).then_inc(done, 1)
    return count + 2


def normalise_chunk(dve, rows, x, scale_rows, centre, c, step, done):
    for j in range(TPC):
        n = c * TPC + j
        last = dve.tensor_scalar(rows[:, j, :], x[:, n, :], centre[:, n, 0:1], scale_rows[:, n:n + 1],
                                 ALU.subtract, ALU.mult)
    last.then_inc(done, 1)


def turn_chunk(pe, turned, rows, ident):
    for kc in range(KC):
        for j in range(TPC):
            last = pe.transpose(turned[:, kc, bass.ts(j, P)], rows[:, j, bass.ts(kc, P)], ident)
    return last


class Steps:

    def __init__(self, eng, sem):
        self.eng, self.sem, self.n = eng, sem, 0

    def then(self, ins):
        self.n += 1
        ins.then_inc(self.sem, 1)
        self.eng.wait_ge(self.sem, self.n)


def rank_experts(dve, chain, logits, before, above, equal, rank):
    shape = [P, NT, EXPERTS, EXPERTS]
    other = logits.unsqueeze(2).to_broadcast(shape)
    own = logits.unsqueeze(3).to_broadcast(shape)
    dve.tensor_tensor(above, other, own, ALU.is_gt)
    chain.then(dve.tensor_tensor(equal, other, own, ALU.is_equal))
    chain.then(dve.tensor_tensor(equal, equal, before.unsqueeze(1).to_broadcast(shape), ALU.mult))
    chain.then(dve.tensor_tensor(above, above, equal, ALU.add))
    chain.then(dve.tensor_reduce(rank, above, AX.X, ALU.add))


def ffn0_front(nc, sem, t, a):
    with ExitStack() as ctx:
        def tile(name, shape, dt=F32):
            return ctx.enter_context(nc.sbuf_tensor(name, shape, dt))

        def bank(name, shape):
            return ctx.enter_context(nc.psum_tensor(name, shape, F32))

        w_raw = tile("f_w_raw", [P, 3, KC, D])
        w_hi = tile("f_w_hi", [P, 3, KC, D], F32R)
        w_lo = tile("f_w_lo", [P, 3, KC, D], F32R)
        gate_raw = tile("f_gate_raw", [P, KC, P])
        gate_hi = tile("f_gate_hi", [P, KC, P], F32R)
        gate_lo = tile("f_gate_lo", [P, KC, P], F32R)
        bias = tile("f_bias", [P, 3, KC])
        rows = tile("f_rows", [P, 2, TPC, D])
        xT_hi = tile("f_xT_hi", [P, 2, KC, CH], F32R)
        xT_lo = tile("f_xT_lo", [P, 2, KC, CH], F32R)
        h_hi = tile("f_h_hi", [P, 2, KC, CH], F32R)
        h_lo = tile("f_h_lo", [P, 2, KC, CH], F32R)
        silu = tile("f_silu", [P, KC, CH])
        gated = tile("f_gated", [P, KC, CH])
        stats = tile("f_stats", [P, NT, 6])
        mean_var = tile("f_mean_var", [P, NT, 2])
        std = tile("f_std", [P, NT])
        rstd = tile("f_rstd", [P, NT])
        logitsT = tile("f_logitsT", [EXPERTS, TOK])
        turned = bank("f_turned", [P, KC, CH])
        hidden = bank("f_hidden", [P, KC, CH])
        gu = bank("f_gu", [P, 2, KC, CH])

        loaded = sem("f_loaded")
        w_loaded = sem("f_w_loaded")
        w_split = sem("f_w_split")
        stats_step = sem("f_stats_step")
        stats_done = sem("f_stats_done")
        std_done = sem("f_std_done")
        rstd_done = sem("f_rstd_done")
        normed = sem("f_normed")
        x_turned = sem("f_x_turned")
        x_hi = sem("f_x_hi")
        x_lo = sem("f_x_lo")
        h_ready = sem("f_h_ready")
        h_hi_done = sem("f_h_hi_done")
        h_lo_done = sem("f_h_lo_done")
        gu_ready = sem("f_gu_ready")
        silu_done = sem("f_silu_done")
        gated_done = sem("f_gated_done")
        s_hi = sem("f_s_hi")
        s_lo = sem("f_s_lo")
        logits_ready = sem("f_logits_ready")
        logits_out = sem("f_logits_out")
        logits_turned = sem("f_logits_turned")
        logits_rows = sem("f_logits_rows")

        block = ctx.enter_context(nc.Block())

        @block.sync
        def _(sp):
            sp.dma_start(bias[:], a["col_bias0"]).then_inc(loaded, 16)
            for n, name in enumerate(("lin0_w", "swi1_w1", "swi1_w2")):
                sp.dma_start(w_raw[:, n], a[name].rearrange("(k p) n -> p k n", p=P)).then_inc(w_loaded, 16)
            sp.dma_start(gate_raw[:], a["gate0"].rearrange("(k p) n -> p k n", p=P)).then_inc(w_loaded, 16)
            sp.dma_start(t["before"][:], a["before"].partition_broadcast(P)).then_inc(loaded, 16)
            for e in range(2):
                sp.dma_start(t["e_raw"][:, e], a["experts0"][e].rearrange("m (k p) n -> p (m k) n", p=P))\
                    .then_inc(t["e_loaded"][e], 16)

        @block.gpsimd
        def _(pool):
            pool.wait_ge(w_loaded, 64)
            n = 0
            for m in range(3):
                n = split_weights(pool, w_raw[:, m], w_hi[:, m], w_lo[:, m], w_split, n)
            split_weights(pool, gate_raw[:], gate_hi[:], gate_lo[:], w_split, n)
            pool.memset(t["combine"][:], 1.0).then_inc(t["ones_set"], 1)
            pool.memset(t["mixed"][:], 0.0).then_inc(t["ones_set"], 1)
            for e in range(2):
                pool.wait_ge(t["e_loaded"][e], 16)
                split_weights(pool, t["e_raw"][:, e], t["e_hi"][:, e], t["e_lo"][:, e], t["e_split"], 2 * e)

        @block.scalar
        def _(act):
            act.wait_ge(stats_done, NT)
            act.activation(std[:], mean_var[:, :, 1], ACT.Sqrt, bias=t["ln_eps"][:]).then_inc(std_done, 1)
            act.wait_ge(loaded, 32)
            for c in range(NCH + 2):
                if c < NCH:
                    act.wait_ge(x_turned, c + 1)
                    act.activation(xT_hi[:, c % 2], turned[:], ACT.Copy).then_inc(x_hi, 1)
                if 1 <= c <= NCH:
                    act.wait_ge(h_ready, c)
                    for m in range(KC):
                        act.activation(h_hi[:, (c - 1) % 2, m, :], hidden[:, m, :], ACT.Identity,
                                       bias=bias[:, 0, m:m + 1]).then_inc(h_hi_done, 1)
                if c >= 2:
                    act.wait_ge(gu_ready, c - 1)
                    act.wait_ge(gated_done, (c - 2) * KC)
                    for m in range(KC):
                        act.activation(silu[:, m, :], gu[:, 0, m, :], ACT.Silu, bias=bias[:, 1, m:m + 1])\
                            .then_inc(silu_done, 1)
                    act.wait_ge(gated_done, (c - 1) * KC)
                    act.activation(t["hT_hi"][:, :, bass.ts(c - 2, CH)], gated[:], ACT.Copy).then_inc(s_hi, 1)
            for c in range(NCH):
                act.wait_ge(logits_ready, c + 1)
                act.activation(logitsT[:, bass.ts(c, CH)], hidden[0:EXPERTS, c % KC, :], ACT.Copy)\
                    .then_inc(logits_out, 1)
            act.wait_ge(logits_turned, 1)
            act.activation(t["logits"][:], turned[:, 0, 0:NT * EXPERTS].rearrange("p (n e) -> p n e", e=EXPERTS),
                           ACT.Copy).then_inc(logits_rows, 1)

        @block.vector
        def _(dve):
            for j in range(NT):
                dve.bn_stats(stats[:, j, :], t["x_res"][:, j, :]).then_inc(stats_step, 1)
            for j in range(NT):
                dve.wait_ge(stats_step, j + 1)
                dve.bn_aggr(mean_var[:, j, :], stats[:, j, :]).then_inc(stats_done, 1)
            dve.wait_ge(std_done, 1)
            dve.reciprocal(rstd[:], std[:]).then_inc(rstd_done, 1)
            dve.wait_ge(rstd_done, 1)
            normalise_chunk(dve, rows[:, 0], t["x_res"], rstd, mean_var, 0, None, normed)
            for c in range(NCH + 2):
                if c + 1 < NCH:
                    dve.wait_ge(x_turned, c)
                    normalise_chunk(dve, rows[:, (c + 1) % 2], t["x_res"], rstd, mean_var, c + 1, None, normed)
                if c < NCH:
                    dve.wait_ge(x_hi, c + 1)
                    dve.tensor_tensor(xT_lo[:, c % 2], turned[:], f32(xT_hi[:, c % 2]), ALU.subtract)\
                        .then_inc(x_lo, 1)
                if 1 <= c <= NCH:
                    for m in range(KC):
                        dve.wait_ge(h_hi_done, (c - 1) * KC + m + 1)
                        dve.scalar_tensor_tensor(h_lo[:, (c - 1) % 2, m, :], hidden[:, m, :], bias[:, 0, m:m + 1],
                                                 f32(h_hi[:, (c - 1) % 2, m, :]), ALU.add, ALU.subtract)\
                            .then_inc(h_lo_done, 1)
                if c >= 2:
                    for m in range(KC):
                        dve.wait_ge(silu_done, (c - 2) * KC + m + 1)
                        dve.wait_ge(s_lo, c - 2)
                        dve.scalar_tensor_tensor(gated[:, m, :], gu[:, 1, m, :], bias[:, 2, m:m + 1],
                                                 silu[:, m, :], ALU.add, ALU.mult).then_inc(gated_done, 1)
                    dve.wait_ge(s_hi, c - 1)
                    dve.tensor_tensor(t["hT_lo"][:, :, bass.ts(c - 2, CH)], gated[:],
                                      f32(t["hT_hi"][:, :, bass.ts(c - 2, CH)]), ALU.subtract).then_inc(s_lo, 1)

        @block.tensor
        def _(pe):
            for c in range(NCH + 2):
                if c < NCH:
                    pe.wait_ge(normed, c + 1)
                    pe.wait_ge(x_lo, c)
                    turn_chunk(pe, turned, rows[:, c % 2], t["ident"][:]).then_inc(x_turned, 1)
                if 1 <= c <= NCH:
                    pe.wait_ge(x_lo, c)
                    pe.wait_ge(w_split, 2)
                    pe.wait_ge(h_lo_done, (c - 1) * KC)
                    r = (c - 1) % 2
                    project_columns(pe, hidden, (w_hi[:, 0], w_lo[:, 0]), (xT_hi[:, r], xT_lo[:, r]))\
                        .then_inc(h_ready, 1)
                if c >= 2:
                    pe.wait_ge(h_lo_done, (c - 1) * KC)
                    pe.wait_ge(w_split, 6)
                    pe.wait_ge(gated_done, (c - 2) * KC)
                    r = c % 2
                    for n in range(2):
                        last = project_columns(pe, gu[:, n], (w_hi[:, 1 + n], w_lo[:, 1 + n]),
                                               (h_hi[:, r], h_lo[:, r]))
                    last.then_inc(gu_ready, 1)
            pe.wait_ge(w_split, 8)
            for c in range(NCH):
                pe.wait_ge(s_lo, c + 1)
                if c >= KC:
                    pe.wait_ge(logits_out, c - KC + 1)
                for kc in range(KC):
                    last = split_products(pe, hidden[:, c % KC, :], (gate_hi[:, kc, :], gate_lo[:, kc, :]),
                                          (t["hT_hi"][:, kc, bass.ts(c, CH)], t["hT_lo"][:, kc, bass.ts(c, CH)]),
                                          kc == 0, kc == KC - 1)
                last.then_inc(logits_ready, 1)
            pe.wait_ge(logits_out, NCH)
            for n in range(NT):
                last = pe.transpose(turned[:, 0, bass.ts(n, EXPERTS)], logitsT[:, bass.ts(n, P)],
                                    t["ident"][0:EXPERTS, 0:EXPERTS])
            last.then_inc(logits_turned, 1)


def mixture(nc, sem, t, weights, parts, shares, top):
    tag = f"m{parts}"
    with ExitStack() as ctx:
        def tile(name, shape, dt=F32):
            return ctx.enter_context(nc.sbuf_tensor(name, shape, dt))

        def bank(name, shape):
            return ctx.enter_context(nc.psum_tensor(name, shape, F32))

        above = tile(tag + "_above", [P, NT, EXPERTS, EXPERTS])
        equal = tile(tag + "_equal", [P, NT, EXPERTS, EXPERTS])
        rank = tile(tag + "_rank", [P, NT, EXPERTS])
        share = tile(tag + "_share", [P, NT, EXPERTS])
        peak = tile(tag + "_peak", [P, NT])
        total = tile(tag + "_total", [P, NT])
        silu = tile(tag + "_silu", [P, KC, CH])
        gated = tile(tag + "_gated", [P, KC, CH])
        g_hi = tile(tag + "_g_hi", [P, 2, KC, CH], F32R)
        g_lo = tile(tag + "_g_lo", [P, 2, KC, CH], F32R)
        gu = bank(tag + "_gu", [P, KC, 2, CH])
        down = bank(tag + "_down", [P, 2, TPC, D])

        chain_sem = sem(tag + "_chain")
        shifted = sem(tag + "_shifted")
        exp_done = sem(tag + "_exp_done")
        gu_ready = sem(tag + "_gu_ready")
        silu_done = sem(tag + "_silu_done")
        gated_done = sem(tag + "_gated_done")
        hi_done = sem(tag + "_hi_done")
        lo_done = sem(tag + "_lo_done")
        down_ready = sem(tag + "_down_ready")
        mixed_done = sem(tag + "_mixed_done")

        block = ctx.enter_context(nc.Block())

        def each_pair(eng, body):
            body(0, True)
            with eng.Fori(1, parts // 2) as i:
                body(i, False)

        @block.sync
        def _(sp):
            def body(i, first):
                for e in range(2):
                    sp.wait_ge(t["e_split"], 4 * (i - 1) + (2 * e + 2))
                    sp.dma_start(t["e_raw"][:, e],
                                 weights[bass.ds(2 * i + e, 1)].rearrange("o m (k p) n -> p (o m k) n", p=P))\
                        .then_inc(t["e_loaded"][e], 16)
            with sp.Fori(1, parts // 2) as i:
                body(i, False)

        @block.gpsimd
        def _(pool):
            with pool.Fori(1, parts // 2) as i:
                for e in range(2):
                    pool.wait_ge(t["e_loaded"][e], 16 * i + 16)
                    pool.wait_ge(down_ready, 2 * NCH * (i - 1) + NCH * (e + 1))
                    held(pool, t)
                    pool.tensor_copy(t["e_hi"][:, e], t["e_raw"][:, e]).then_inc(t["e_split"], 1)
                    pool.wait_ge(t["e_split"], 4 * i + (2 * e + 1))
                    pool.tensor_tensor(t["e_lo"][:, e], t["e_raw"][:, e], f32(t["e_hi"][:, e]), ALU.subtract)\
                        .then_inc(t["e_split"], 1)

        @block.scalar
        def _(act):
            act.wait_ge(shifted, 1)
            act.activation(share[:], share[:], ACT.Exp).then_inc(exp_done, 1)

            def body(i, first):
                for k in range(2 * NCH):
                    n = 2 * NCH * i + k
                    for m in range(KC):
                        act.wait_ge(gu_ready, 2 * n + (m + 1))
                        if not (first and k == 0):
                            act.wait_ge(gated_done, 2 * n + (m - 1))
                        act.activation(silu[:, m, :], gu[:, m, 0, :], ACT.Silu).then_inc(silu_done, 1)
                        act.wait_ge(gated_done, 2 * n + (m + 1))
                        if not (first and k < 2):
                            act.wait_ge(down_ready, n - 1)
                        act.activation(g_hi[:, k % 2, m, :], gated[:, m, :], ACT.Copy).then_inc(hi_done, 1)

            each_pair(act, body)

        @block.vector
        def _(dve):
            chain = Steps(dve, chain_sem)
            shape = [P, NT, EXPERTS]
            chain.then(dve.tensor_reduce(peak[:], t["logits"][:], AX.X, ALU.max))
            dve.tensor_tensor(share[:], t["logits"][:], peak[:].unsqueeze(2).to_broadcast(shape), ALU.subtract)\
                .then_inc(shifted, 1)
            rank_experts(dve, chain, t["logits"][:], t["before"][:].rearrange("p (i j) -> p i j", j=EXPERTS),
                         above[:], equal[:], rank[:])
            chain.then(dve.tensor_scalar(rank[:], rank[:], float(top), None, ALU.is_lt))
            dve.wait_ge(exp_done, 1)
            chain.then(dve.tensor_tensor(share[:], share[:], rank[:], ALU.mult))
            chain.then(dve.tensor_reduce(total[:], share[:], AX.X, ALU.add))
            chain.then(dve.reciprocal(total[:], total[:]))
            if t["ones_set"] is not None:
                dve.wait_ge(t["ones_set"], 2)
            for n in range(shares):
                chain.then(dve.tensor_tensor(
                    t["combine"][:, :, 0:EXPERTS * shares].rearrange("p n (e s) -> p n e s", s=shares)[:, :, :, n],
                    share[:], total[:].unsqueeze(2).to_broadcast(shape), ALU.mult))

            def mix(i, k):
                e, c = divmod(k, NCH)
                n = 2 * NCH * i + k
                dve.wait_ge(down_ready, n + 1)
                for j in range(TPC):
                    r = c * TPC + j
                    last = dve.scalar_tensor_tensor(
                        t["mixed"][:, r, :], down[:, k % 2, j, :],
                        t["combine"][:, r, bass.ds(2 * i + e, 1)], t["mixed"][:, r, :], ALU.mult, ALU.add)
                last.then_inc(mixed_done, 1)

            def body(i, first):
                for k in range(2 * NCH):
                    n = 2 * NCH * i + k
                    for m in range(KC):
                        dve.wait_ge(silu_done, 2 * n + (m + 1))
                        if not (first and k == 0):
                            dve.wait_ge(lo_done, 2 * n + (m - 1))
                        dve.tensor_tensor(gated[:, m, :], gu[:, m, 1, :], silu[:, m, :], ALU.mult)\
                            .then_inc(gated_done, 1)
                        dve.wait_ge(hi_done, 2 * n + (m + 1))
                        dve.tensor_tensor(g_lo[:, k % 2, m, :], gated[:, m, :], f32(g_hi[:, k % 2, m, :]),
                                          ALU.subtract).then_inc(lo_done, 1)
                    if k >= 1:
                        mix(i, k - 1)
                    elif not first:
                        mix(i - 1, 2 * NCH - 1)

            each_pair(dve, body)
            mix(parts // 2 - 1, 2 * NCH - 1)

        @block.tensor
        def _(pe):
            def gate_up(i, k, first):
                e, c = divmod(k, NCH)
                n = 2 * NCH * i + k
                if c == 0:
                    pe.wait_ge(t["e_split"], 4 * i + (2 * e + 2))
                for m in range(KC):
                    if not (first and k == 0):
                        pe.wait_ge(gated_done, 2 * n + (m - 1))
                    for w in range(2):
                        for kc in range(KC):
                            last = split_products(
                                pe, gu[:, m, w, :],
                                (t["e_hi"][:, e, 2 * w + kc, bass.ts(m, P)], t["e_lo"][:, e, 2 * w + kc, bass.ts(m, P)]),
                                (t["hT_hi"][:, kc, bass.ts(c, CH)], t["hT_lo"][:, kc, bass.ts(c, CH)]),
                                kc == 0, kc == KC - 1)
                    last.then_inc(gu_ready, 1)

            def down_rows(i, k, first):
                e, c = divmod(k, NCH)
                n = 2 * NCH * i + k
                pe.wait_ge(lo_done, 2 * n + 2)
                if not (first and k < 2):
                    pe.wait_ge(mixed_done, n - 1)
                for j in range(TPC):
                    for m in range(KC):
                        last = split_products(
                            pe, down[:, k % 2, j, :],
                            (g_hi[:, k % 2, m, bass.ts(j, P)], g_lo[:, k % 2, m, bass.ts(j, P)]),
                            (t["e_hi"][:, e, 4 + m, :], t["e_lo"][:, e, 4 + m, :]), m == 0, m == KC - 1)
                last.then_inc(down_ready, 1)

            def body(i, first):
                for k in range(2 * NCH):
                    gate_up(i, k, first)
                    if k >= 1:
                        down_rows(i, k - 1, first)
                    elif not first:
                        down_rows(i - 1, 2 * NCH - 1, False)

            each_pair(pe, body)
            down_rows(parts // 2 - 1, 2 * NCH - 1, False)


def ffn0_back(nc, sem, t, a):
    with ExitStack() as ctx:
        def tile(name, shape, dt=F32):
            return ctx.enter_context(nc.sbuf_tensor(name, shape, dt))

        def bank(name, shape):
            return ctx.enter_context(nc.psum_tensor(name, shape, F32))

        w_raw = tile("g_w_raw", [P, 3, KC, D])
        w_hi = tile("g_w_hi", [P, 3, KC, D], F32R)
        w_lo = tile("g_w_lo", [P, 3, KC, D], F32R)
        bias = tile("g_bias", [P, KC])
        row_bias = tile("g_row_bias", [P, 2, D])
        xT_hi = tile("g_xT_hi", [P, 2, KC, CH], F32R)
        xT_lo = tile("g_xT_lo", [P, 2, KC, CH], F32R)
        h_hi = tile("g_h_hi", [P, 2, KC, CH], F32R)
        h_lo = tile("g_h_lo", [P, 2, KC, CH], F32R)
        biased = tile("g_biased", [P, TPC, 2, D])
        silu = tile("g_silu", [P, TPC, D])
        gated = tile("g_gated", [P, TPC, D])
        turned = bank("g_turned", [P, KC, CH])
        hidden = bank("g_hidden", [P, KC, CH])
        gu = bank("g_gu", [P, TPC, 2, D])

        loaded = sem("g_loaded")
        w_split = sem("g_w_split")
        x_turned = sem("g_x_turned")
        x_hi = sem("g_x_hi")
        x_lo = sem("g_x_lo")
        h_ready = sem("g_h_ready")
        h_hi_done = sem("g_h_hi_done")
        h_lo_done = sem("g_h_lo_done")
        gu_ready = sem("g_gu_ready")
        biased_done = sem("g_biased_done")
        silu_done = sem("g_silu_done")
        gated_done = sem("g_gated_done")
        added = sem("g_added")

        block = ctx.enter_context(nc.Block())

        @block.sync
        def _(sp):
            for n, name in enumerate(("lin1_w", "swi2_w1", "swi2_w2")):
                dst = w_raw[:, 0] if n == 0 else w_raw[:, 1:3].rearrange("p m k n -> p (m k n)")\
                    .rearrange("p (k m n) -> p k m n", k=KC, m=2)[:, :, n - 1]
                sp.dma_start(dst, a[name].rearrange("(k p) n -> p k n", p=P)).then_inc(loaded, 16)
            sp.dma_start(bias[:], a["col_bias1"]).then_inc(loaded, 16)
            for n, name in enumerate(("swi2_b1", "swi2_b2")):
                sp.dma_start(row_bias[:, n], a[name].partition_broadcast(P)).then_inc(loaded, 16)

        @block.gpsimd
        def _(pool):
            pool.wait_ge(loaded, 96)
            n = split_weights(pool, w_raw[:, 0], w_hi[:, 0], w_lo[:, 0], w_split, 0)
            split_weights(pool, w_raw[:, 1:3], w_hi[:, 1:3], w_lo[:, 1:3], w_split, n)
            for n in range(NT):
                pool.wait_ge(gated_done, n + 1)
                pool.tensor_tensor(t["x_res"][:, n, :], t["x_res"][:, n, :], gated[:, n % TPC, :], ALU.add)\
                    .then_inc(added, 1)

        @block.scalar
        def _(act):
            act.wait_ge(loaded, 96)
            for c in range(NCH + 2):
                if c < NCH:
                    act.wait_ge(x_turned, c + 1)
                    act.activation(xT_hi[:, c % 2], turned[:], ACT.Copy).then_inc(x_hi, 1)
                if 1 <= c <= NCH:
                    act.wait_ge(h_ready, c)
                    for m in range(KC):
                        act.activation(h_hi[:, (c - 1) % 2, m, :], hidden[:, m, :], ACT.Identity,
                                       bias=bias[:, m:m + 1]).then_inc(h_hi_done, 1)
                if c >= 2:
                    for j in range(TPC):
                        n = (c - 2) * TPC + j
                        act.wait_ge(biased_done, n + 1)
                        if n >= TPC:
                            act.wait_ge(gated_done, n - TPC + 1)
                        act.activation(silu[:, j, :], biased[:, j, 0, :], ACT.Silu).then_inc(silu_done, 1)

        @block.vector
        def _(dve):
            dve.wait_ge(loaded, 96)
            for c in range(NCH + 2):
                if c < NCH:
                    dve.wait_ge(x_hi, c + 1)
                    dve.tensor_tensor(xT_lo[:, c % 2], turned[:], f32(xT_hi[:, c % 2]), ALU.subtract)\
                        .then_inc(x_lo, 1)
                if 1 <= c <= NCH:
                    for m in range(KC):
                        dve.wait_ge(h_hi_done, (c - 1) * KC + m + 1)
                        dve.scalar_tensor_tensor(h_lo[:, (c - 1) % 2, m, :], hidden[:, m, :], bias[:, m:m + 1],
                                                 f32(h_hi[:, (c - 1) % 2, m, :]), ALU.add, ALU.subtract)\
                            .then_inc(h_lo_done, 1)
                if c >= 2:
                    for j in range(TPC + 1):
                        n = (c - 2) * TPC + j
                        if j < TPC:
                            dve.wait_ge(gu_ready, n + 1)
                            if n >= TPC:
                                dve.wait_ge(silu_done, n - TPC + 1)
                            dve.tensor_tensor(biased[:, j], gu[:, j], row_bias[:], ALU.add)\
                                .then_inc(biased_done, 1)
                        if j >= 1:
                            dve.wait_ge(silu_done, n)
                            if n > TPC:
                                dve.wait_ge(added, n - TPC)
                            dve.tensor_tensor(gated[:, j - 1, :], silu[:, j - 1, :], biased[:, j - 1, 1, :],
                                              ALU.mult).then_inc(gated_done, 1)

        @block.tensor
        def _(pe):
            for c in range(NCH + 2):
                if c < NCH:
                    pe.wait_ge(x_lo, c)
                    turn_chunk(pe, turned, t["mixed"][:, c * TPC:(c + 1) * TPC], t["ident"][:])\
                        .then_inc(x_turned, 1)
                if 1 <= c <= NCH:
                    pe.wait_ge(x_lo, c)
                    pe.wait_ge(w_split, 2)
                    pe.wait_ge(h_lo_done, (c - 1) * KC)
                    r = (c - 1) % 2
                    project_columns(pe, hidden, (w_hi[:, 0], w_lo[:, 0]), (xT_hi[:, r], xT_lo[:, r]))\
                        .then_inc(h_ready, 1)
                if c >= 2:
                    pe.wait_ge(h_lo_done, (c - 1) * KC)
                    pe.wait_ge(w_split, 4)
                    r = c % 2
                    both = [w[:, 1:3].rearrange("p m k n -> p (m k n)").rearrange("p (k n) -> p k n", k=KC)
                            for w in (w_hi, w_lo)]
                    for j in range(TPC):
                        n = (c - 2) * TPC + j
                        if n >= TPC:
                            pe.wait_ge(biased_done, n - TPC + 1)
                        for kc in range(KC):
                            last = split_products(
                                pe, gu[:, j].rearrange("p m n -> p (m n)"),
                                (h_hi[:, r, kc, bass.ts(j, P)], h_lo[:, r, kc, bass.ts(j, P)]),
                                (both[0][:, kc, :], both[1][:, kc, :]), kc == 0, kc == KC - 1)
                        last.then_inc(gu_ready, 1)


Q_HEADS, Q_HD = 4, 64
RMS_EPS = 1e-6


def attention1(nc, sem, t, a):
    with ExitStack() as ctx:
        def tile(name, shape, dt=F32):
            return ctx.enter_context(nc.sbuf_tensor(name, shape, dt))

        def bank(name, shape):
            return ctx.enter_context(nc.psum_tensor(name, shape, F32))

        ctx_rows = tile("c_ctx_rows", [P, NT, D])
        wq = [tile(f"c_wq_{n}", [P, KC, 2 * D], d) for n, d in (("raw", F32), ("hi", F32R), ("lo", F32R))]
        wkv = [tile(f"c_wkv_{n}", [P, KC, D], d) for n, d in (("raw", F32), ("hi", F32R), ("lo", F32R))]
        wo = [tile(f"c_wo_{n}", [P, KC, D], d) for n, d in (("raw", F32), ("hi", F32R), ("lo", F32R))]
        rope = tile("c_rope", [P, 4, ST, Q_HD])
        mask_words = tile("c_mask_words", [P, TOK // 4], I32)
        key_bias = tile("c_key_bias", [P, B, S], F32R)
        all_masked = tile("c_all_masked", [P, B])
        scale = tile("c_scale", [P, B])
        neg_scale = tile("c_neg_scale", [P, B])
        depth = tile("c_depth", [P, B])
        mean_f = tile("c_mean_f", [P, P])
        mean_r = tile("c_mean_r", [P, P], F32R)
        gain = tile("c_gain", [P, KC])
        rms_eps = tile("c_rms_eps", [P, 1])
        stats = tile("c_stats", [P, 2, NT, 6])
        mean_var = tile("c_mean_var", [P, 2, NT, 2])
        work = tile("c_work", [P, 4, NT])
        row_scale = tile("c_row_scale", [P, 2, NT])
        rows = tile("c_rows", [P, 2, ST, D])
        pT_hi = tile("c_pT_hi", [P, 2, KC, S], F32R)
        pT_lo = tile("c_pT_lo", [P, 2, KC, S], F32R)
        k_parts = tile("c_k_parts", [P, 2, ST, Q_HD])
        k_full = tile("c_k_full", [P, ST, Q_HD])
        k_rows = tile("c_k_rows", [P, ST, 2, 2, Q_HD], F32R)
        q_parts = tile("c_q_parts", [P, 2, ST, D])
        q_full = tile("c_q_full", [P, ST, Q_HEADS, Q_HD])
        q_rows = tile("c_q_rows", [P, ST, Q_HEADS, 2, Q_HD], F32R)
        kT = tile("c_kT", [P, 2, S], F32R)
        qT = tile("c_qT", [P, Q_HEADS, S], F32R)
        v_rows = tile("c_v_rows", [P, 2, ST, Q_HD])
        peak = tile("c_peak", [P, 2, ST])
        shift = tile("c_shift", [P, 2, ST])
        total = tile("c_total", [P, 2, ST])
        total_inv = tile("c_total_inv", [P, 2, ST])
        weights = tile("c_weights", [P, 2, ST, S])
        normed_w = tile("c_normed_w", [P, 2, ST, S])
        weightsT = tile("c_weightsT", [P, 2, ST, S])
        eT_hi = tile("c_eT_hi", [P, KC, S], F32R)
        eT_lo = tile("c_eT_lo", [P, KC, S], F32R)
        turned = bank("c_turned", [P, KC, S])
        kv = bank("c_kv", [P, ST, D])
        qq = bank("c_qq", [P, ST, 2, D])
        scores = bank("c_scores", [P, 2, ST, S])
        wT = bank("c_wT", [P, ST, S])
        values = bank("c_values", [P, KC, S])

        names = ("stats_done ctx_scale loaded w_loaded ctx_loaded w_split mean_set masked_found none_found scaled step_d step_a "
                 "rows_ready turned_ready split_hi split_lo kv_ready q_ready k_roped q_roped "
                 "pool_step k_rows_ready q_rows_ready v_copied k_turned k_copied q_turned q_copied s_ready "
                 "peak_found shift_ready w_ready inv_ready w_normed w_turned wT_copied pv_ready "
                 "e_hi e_lo o_ready res_added").split()
        s = {n: sem("c_" + n) for n in names}

        block = ctx.enter_context(nc.Block())

        def steps(eng, step):
            step(-1, True, False, False)
            step(0, True, True, False)
            with eng.Fori(0, B // 2 - 1) as i:
                for p in range(2):
                    step(2 * i + (1 + p), True, True, True, parity=(1 + p) % 2)
            step(B - 1, False, True, True)
            step(B, False, False, True)

        @block.sync
        def _(sp):
            sp.dma_start(rope[:], a["rope"]).then_inc(s["loaded"], 16)
            sp.dma_start(gain[:], a["rms_gain"]).then_inc(s["loaded"], 16)
            sp.dma_start(ctx_rows[:], a["ctx"].rearrange("(j p) d -> p j d", p=P)).then_inc(s["ctx_loaded"], 16)
            sp.dma_start(mask_words[:], a["mask1"].partition_broadcast(P))\
                .then_inc(s["loaded"], 16)
            for w, name in ((wkv, "wkv1"), (wq, "wq1"), (wo, "wo1")):
                sp.dma_start(w[0][:], a[name].rearrange("(k p) n -> p k n", p=P)).then_inc(s["w_loaded"], 16)

        @block.gpsimd
        def _(pool):
            pool.memset(rms_eps[:], RMS_EPS).then_inc(s["mean_set"], 1)
            pool.memset(mean_f[:], 1.0 / P).then_inc(s["mean_set"], 1)
            pool.wait_ge(s["mean_set"], 2)
            pool.tensor_copy(mean_r[:], mean_f[:]).then_inc(s["mean_set"], 1)
            pool.wait_ge(s["w_loaded"], 48)
            n = 0
            for w in (wkv, wq):
                n = split_weights(pool, w[0][:], w[1][:], w[2][:], s["w_split"], n)
            pool.wait_ge(s["loaded"], 48)
            pool.tensor_scalar(key_bias[:], mask_words[:].bitcast(U8).rearrange("p (b k) -> p b k", b=B), 0, None, ALU.is_equal).then_inc(s["masked_found"], 1)
            pool.wait_ge(s["none_found"], 1)
            for out, factor in ((scale, -Q_HD ** -0.5), (neg_scale, Q_HD ** -0.5), (depth, MASKED)):
                pool.tensor_scalar(out[:], all_masked[:], -1.0, factor, ALU.add, ALU.mult).then_inc(s["scaled"], 1)
            pool.wait_ge(s["scaled"], 3)
            pool.tensor_tensor(key_bias[:], f32(key_bias[:]), depth[:].unsqueeze(2).to_broadcast([P, B, S]),
                               ALU.mult).then_inc(s["scaled"], 1)
            split_weights(pool, wo[0][:], wo[1][:], wo[2][:], s["w_split"], n)

            def split_rows(f, parts, full, out_hi, out_lo, own, roped, turned_sem, done, first):
                pool.wait_ge(s[roped], f + 1)
                pool.tensor_tensor(full, parts[0], parts[1], ALU.add).then_inc(s["pool_step"], 1)
                if not first:
                    pool.wait_ge(s[turned_sem], f)
                pool.wait_ge(s["pool_step"], 4 * f + own + 1)
                held(pool, t)
                pool.tensor_copy(out_hi[0], out_hi[1]).then_inc(s["pool_step"], 1)
                pool.wait_ge(s["pool_step"], 4 * f + own + 2)
                pool.tensor_tensor(out_lo[0], out_lo[1], out_lo[2], ALU.subtract).then_inc(s[done], 1)

            def k_split(f, first):
                full = k_full[:].unsqueeze(2).to_broadcast([P, ST, 2, Q_HD])
                split_rows(f, (k_parts[:, 0], k_parts[:, 1]), k_full[:], (k_rows[:, :, 0], full),
                           (k_rows[:, :, 1], full, f32(k_rows[:, :, 0])), 0, "k_roped", "k_turned",
                           "k_rows_ready", first)

            def q_split(f, first):
                split_rows(f, (q_parts[:, 0], q_parts[:, 1]), q_full[:].rearrange("p s h d -> p s (h d)"),
                           (q_rows[:, :, :, 0, :], q_full[:]),
                           (q_rows[:, :, :, 1, :], q_full[:], f32(q_rows[:, :, :, 0, :])), 2, "q_roped",
                           "q_turned", "q_rows_ready", first)

            def norm_weights(b, h, first):
                pool.wait_ge(s["inv_ready"], b * Q_HEADS + (h + 1))
                if not (first and h < 2):
                    pool.wait_ge(s["w_turned"], b * Q_HEADS + (h - 1))
                pool.tensor_tensor(normed_w[:, h % 2], weights[:, h % 2],
                                   total_inv[:, h % 2].unsqueeze(2).to_broadcast([P, ST, S]), ALU.mult)\
                    .then_inc(s["w_normed"], 1)

            def step(b, front, att, prev, parity=None):
                if att:
                    norm_weights(b, 0, not prev)
                if front:
                    k_split(b + 1, not att)
                if att:
                    norm_weights(b, 1, not prev)
                if front:
                    q_split(b + 1, not att)
                if att:
                    norm_weights(b, 2, not prev)
                    norm_weights(b, 3, not prev)

            steps(pool, step)

        @block.scalar
        def _(act):
            act.wait_ge(s["mean_set"], 1)
            act.wait_ge(s["step_d"], 2)
            act.activation(work[:, 0], work[:, 0], ACT.Sqrt, bias=rms_eps[:]).then_inc(s["step_a"], 1)
            act.activation(work[:, 1], mean_var[:, 1, :, 1], ACT.Sqrt, bias=t["ln_eps"][:]).then_inc(s["step_a"], 1)
            act.wait_ge(s["step_d"], 5)
            act.activation(work[:, 2], work[:, 2], ACT.Sqrt, bias=rms_eps[:]).then_inc(s["step_a"], 1)

            def high_parts(f, src):
                act.wait_ge(s["turned_ready"], 2 * f + (src + 1))
                for kc in range(KC):
                    last = act.activation(pT_hi[:, src, kc, :], turned[:, kc, :], ACT.Copy,
                                          scale=gain[:, kc:kc + 1])
                last.then_inc(s["split_hi"], 1)

            def exps(b, h, first):
                act.wait_ge(s["shift_ready"], b * Q_HEADS + (h + 1))
                if not (first and h < 2):
                    act.wait_ge(s["w_normed"], b * Q_HEADS + (h - 1))
                held(act, t)
                for q in range(ST):
                    last = act.activation(weights[:, h % 2, q, :], scores[:, h % 2, q, :], ACT.Exp,
                                          bias=shift[:, h % 2, q:q + 1], scale=scale[:, bass.ds(b, 1)],
                                          accum_out=total[:, h % 2, q:q + 1])
                last.then_inc(s["w_ready"], 1)

            def step(b, front, att, prev, parity=None):
                f = b + 1
                if att:
                    exps(b, 0, not prev)
                    exps(b, 1, not prev)
                if front:
                    r = (parity + 1) % 2 if parity is not None else f % 2
                    high_parts(f, 0)
                    act.wait_ge(s["k_roped"], f + 1)
                    if prev:
                        act.wait_ge(s["pv_ready"], (b - 1) * Q_HEADS + Q_HEADS)
                    act.activation(v_rows[:, r], kv[:, :, 2 * Q_HD:3 * Q_HD], ACT.Copy).then_inc(s["v_copied"], 1)
                    high_parts(f, 1)
                if att:
                    exps(b, 2, not prev)
                    exps(b, 3, not prev)
                if front:
                    act.wait_ge(s["k_turned"], f + 1)
                    act.activation(kT[:], kv[:], ACT.Copy).then_inc(s["k_copied"], 1)
                    act.wait_ge(s["q_turned"], f + 1)
                    act.activation(qT[:], qq[:].rearrange("p s w d -> p (s w d)").rearrange("p (h t) -> p h t", h=Q_HEADS),
                                   ACT.Copy).then_inc(s["q_copied"], 1)
                if att:
                    act.wait_ge(s["pv_ready"], b * Q_HEADS + Q_HEADS)
                    if prev:
                        act.wait_ge(s["o_ready"], b)
                    act.activation(eT_hi[:], values[:], ACT.Copy).then_inc(s["e_hi"], 1)

            steps(act, step)

        @block.vector
        def _(dve):
            dve.wait_ge(s["ctx_loaded"], 16)
            for n, x in ((0, ctx_rows), (1, t["x_res"])):
                for j in range(NT):
                    dve.bn_stats(stats[:, n, j, :], x[:, j, :]).then_inc(s["stats_done"], 1)
            for n in range(2):
                for j in range(NT):
                    dve.wait_ge(s["stats_done"], n * NT + j + 1)
                    dve.bn_aggr(mean_var[:, n, j, :], stats[:, n, j, :]).then_inc(s["stats_done"], 1)
            dve.wait_ge(s["stats_done"], 4 * NT)
            d = Steps(dve, s["step_d"])
            d.then(dve.tensor_tensor(work[:, 0], mean_var[:, 0, :, 0], mean_var[:, 0, :, 0], ALU.mult))
            d.then(dve.tensor_tensor(work[:, 0], work[:, 0], mean_var[:, 0, :, 1], ALU.add))
            dve.wait_ge(s["step_a"], 2)
            dve.reciprocal(row_scale[:, 0], work[:, 0]).then_inc(s["ctx_scale"], 1)
            d.then(dve.reciprocal(work[:, 1], work[:, 1]))
            d.then(dve.tensor_tensor(work[:, 2], mean_var[:, 1, :, 1], work[:, 1], ALU.mult))
            d.then(dve.tensor_tensor(work[:, 2], work[:, 2], work[:, 1], ALU.mult))
            dve.wait_ge(s["step_a"], 3)
            d.then(dve.reciprocal(work[:, 3], work[:, 2]))
            d.then(dve.tensor_tensor(row_scale[:, 1], work[:, 3], work[:, 1], ALU.mult))
            dve.wait_ge(s["loaded"], 48)
            dve.wait_ge(s["masked_found"], 1)
            dve.tensor_reduce(all_masked[:], f32(key_bias[:]), AX.X, ALU.min).then_inc(s["none_found"], 1)
            d.then(dve.tensor_scalar(gain[:], gain[:], 1.0, None, ALU.add))
            dve.wait_ge(s["ctx_scale"], 1)

            def norm_rows(f, src, first):
                if not first:
                    dve.wait_ge(s["turned_ready"], 2 * f + (src - 1))
                for j in range(ST):
                    n = bass.ds(f * ST + j, 1)
                    if src == 0:
                        last = dve.tensor_scalar(rows[:, 0, j, :], ctx_rows[:, n, :].rearrange("p o d -> p (o d)"),
                                                 row_scale[:, 0, n], None, ALU.mult)
                    else:
                        last = dve.tensor_scalar(rows[:, 1, j, :], t["x_res"][:, n, :].rearrange("p o d -> p (o d)"),
                                                 mean_var[:, 1, n, 0], row_scale[:, 1, n], ALU.subtract, ALU.mult)
                last.then_inc(s["rows_ready"], 1)

            def low_parts(f, src):
                dve.wait_ge(s["split_hi"], 2 * f + (src + 1))
                for kc in range(KC):
                    last = dve.scalar_tensor_tensor(pT_lo[:, src, kc, :], turned[:, kc, :], gain[:, kc:kc + 1],
                                                    f32(pT_hi[:, src, kc, :]), ALU.mult, ALU.subtract)
                last.then_inc(s["split_lo"], 1)

            def peaks(b, h):
                dve.wait_ge(s["s_ready"], b * Q_HEADS + (h + 1))
                dve.tensor_reduce(peak[:, h % 2], scores[:, h % 2], AX.X, ALU.max).then_inc(s["peak_found"], 1)
                dve.wait_ge(s["peak_found"], b * Q_HEADS + (h + 1))
                dve.tensor_scalar(shift[:, h % 2], peak[:, h % 2], neg_scale[:, bass.ds(b, 1)], None, ALU.mult)\
                    .then_inc(s["shift_ready"], 1)

            def totals(b, h, first):
                dve.wait_ge(s["w_ready"], b * Q_HEADS + (h + 1))
                if not (first and h < 2):
                    dve.wait_ge(s["w_normed"], b * Q_HEADS + (h - 1))
                dve.reciprocal(total_inv[:, h % 2], total[:, h % 2]).then_inc(s["inv_ready"], 1)

            def copy_wT(b, h, first):
                dve.wait_ge(s["w_turned"], b * Q_HEADS + (h + 1))
                if not (first and h < 2):
                    dve.wait_ge(s["pv_ready"], b * Q_HEADS + (h - 1))
                dve.tensor_copy(weightsT[:, h % 2], wT[:]).then_inc(s["wT_copied"], 1)

            def rotate_k(f, first):
                dve.wait_ge(s["kv_ready"], f + 1)
                if not first:
                    dve.wait_ge(s["k_rows_ready"], f)
                dve.tensor_tensor(k_parts[:, 0], kv[:, :, 0:Q_HD], rope[:, 2], ALU.mult)
                dve.tensor_tensor(k_parts[:, 1], kv[:, :, Q_HD:2 * Q_HD], rope[:, 3], ALU.mult)\
                    .then_inc(s["k_roped"], 1)

            def rotate_q(f, first):
                dve.wait_ge(s["q_ready"], f + 1)
                if not first:
                    dve.wait_ge(s["q_rows_ready"], f)
                for w in range(2):
                    last = dve.tensor_tensor(
                        q_parts[:, w].rearrange("p s (h d) -> p s h d", h=Q_HEADS),
                        qq[:, :, w, :].rearrange("p s (h d) -> p s h d", h=Q_HEADS),
                        rope[:, w].unsqueeze(2).to_broadcast([P, ST, Q_HEADS, Q_HD]), ALU.mult)
                last.then_inc(s["q_roped"], 1)

            def step(b, front, att, prev, parity=None):
                f, first = b + 1, not prev
                if prev:
                    dve.wait_ge(s["e_hi"], b)
                    dve.tensor_tensor(eT_lo[:], values[:], f32(eT_hi[:]), ALU.subtract).then_inc(s["e_lo"], 1)
                if front:
                    norm_rows(f, 0, not att)
                if att:
                    peaks(b, 0)
                if front:
                    norm_rows(f, 1, not att)
                if att:
                    peaks(b, 1)
                if front:
                    low_parts(f, 0)
                if att:
                    totals(b, 0, first)
                if prev:
                    dve.wait_ge(s["o_ready"], b)
                    dve.tensor_tensor(t["x_res"][:, bass.ds((b - 1) * ST, ST), :], values[:],
                                      t["x_res"][:, bass.ds((b - 1) * ST, ST), :], ALU.add)\
                        .then_inc(s["res_added"], 1)
                if att:
                    copy_wT(b, 0, first)
                if front:
                    rotate_k(f, not att)
                    low_parts(f, 1)
                if att:
                    totals(b, 1, first)
                    peaks(b, 2)
                if front:
                    rotate_q(f, not att)
                if att:
                    copy_wT(b, 1, first)
                    peaks(b, 3)
                    totals(b, 2, first)
                    copy_wT(b, 2, first)
                    totals(b, 3, first)
                    copy_wT(b, 3, first)

            steps(dve, step)

        @block.tensor
        def _(pe):
            def turn(f, src):
                pe.wait_ge(s["rows_ready"], 2 * f + (src + 1))
                pe.wait_ge(s["split_lo"], 2 * f + src)
                for kc in range(KC):
                    for j in range(ST):
                        last = pe.transpose(turned[:, kc, bass.ts(j, P)], rows[:, src, j, bass.ts(kc, P)], t["ident"][:])
                last.then_inc(s["turned_ready"], 1)

            def project(f, src, w, out, done, free):
                pe.wait_ge(s["split_lo"], 2 * f + (src + 1))
                pe.wait_ge(s[free], f)
                for j in range(ST):
                    for kc in range(KC):
                        last = split_products(
                            pe, out[j], (pT_hi[:, src, kc, bass.ts(j, P)], pT_lo[:, src, kc, bass.ts(j, P)]),
                            (w[1][:, kc, :], w[2][:, kc, :]), kc == 0, kc == KC - 1)
                last.then_inc(s[done], 1)

            def head_scores(b, h, first):
                if h == 0:
                    pe.wait_ge(s["k_copied"], b + 1)
                    pe.wait_ge(s["q_copied"], b + 1)
                if not (first and h < 2):
                    pe.wait_ge(s["w_ready"], b * Q_HEADS + (h - 1))
                for q in range(ST):
                    out = scores[:, h % 2, q, :]
                    pe.matmul(out, mean_r[:], key_bias[:, bass.ds(b, 1), :].rearrange("p o k -> p (o k)"),
                              start=True, stop=False)
                    for part in range(2):
                        last = pe.matmul(out, qT[:, h, bass.ts(q, P)], kT[:, part, :], start=False, stop=part == 1)
                last.then_inc(s["s_ready"], 1)

            def turn_weights(b, h):
                pe.wait_ge(s["w_normed"], b * Q_HEADS + (h + 1))
                pe.wait_ge(s["wT_copied"], b * Q_HEADS + h)
                for k in range(ST):
                    for q in range(ST):
                        last = pe.transpose(wT[:, k, bass.ts(q, P)], normed_w[:, h % 2, q, bass.ts(k, P)], t["ident"][:])
                last.then_inc(s["w_turned"], 1)

            def head_values(b, h, r):
                pe.wait_ge(s["wT_copied"], b * Q_HEADS + (h + 1))
                if h == 0:
                    pe.wait_ge(s["v_copied"], b + 1)
                    pe.wait_ge(s["res_added"], b)
                half = Q_HD * (h % 2)
                for k in range(ST):
                    last = pe.matmul(values[half:half + Q_HD, h // 2, :], v_rows[:, r, k, :], weightsT[:, h % 2, k, :],
                                     start=(k == 0), stop=(k == ST - 1))
                last.then_inc(s["pv_ready"], 1)

            pe.wait_ge(s["w_split"], 4)
            pe.wait_ge(s["mean_set"], 3)

            def step(b, front, att, prev, parity=None):
                f, first = b + 1, not prev
                r = parity if parity is not None else b % 2
                if att:
                    if first:
                        pe.wait_ge(s["scaled"], 4)
                    head_scores(b, 0, first)
                    head_scores(b, 1, first)
                if front:
                    turn(f, 0)
                if prev:
                    pe.wait_ge(s["e_lo"], b)
                    pe.wait_ge(s["w_split"], 6)
                    for j in range(ST):
                        for kc in range(KC):
                            last = split_products(pe, values[:, j, :],
                                                  (eT_hi[:, kc, bass.ts(j, P)], eT_lo[:, kc, bass.ts(j, P)]),
                                                  (wo[1][:, kc, :], wo[2][:, kc, :]), kc == 0, kc == KC - 1)
                    last.then_inc(s["o_ready"], 1)
                if att:
                    turn_weights(b, 0)
                if front:
                    project(f, 0, wkv, [kv[:, j, :] for j in range(ST)], "kv_ready", "k_copied")
                    turn(f, 1)
                if att:
                    head_scores(b, 2, first)
                    head_values(b, 0, r)
                if front:
                    project(f, 1, wq, [qq[:, j].rearrange("p w d -> p (w d)") for j in range(ST)],
                            "q_ready", "q_copied")
                if att:
                    turn_weights(b, 1)
                    head_scores(b, 3, first)
                    head_values(b, 1, r)
                if front:
                    pe.wait_ge(s["k_rows_ready"], f + 1)
                    pe.wait_ge(s["v_copied"], f + 1)
                    for part in range(2):
                        for j in range(ST):
                            last = pe.transpose(kv[:, part, bass.ts(j, P)],
                                                f32(k_rows[:, j, part]).rearrange("p w d -> p (w d)"), t["ident"][:])
                    last.then_inc(s["k_turned"], 1)
                if att:
                    turn_weights(b, 2)
                    head_values(b, 2, r)
                if front:
                    pe.wait_ge(s["q_rows_ready"], f + 1)
                    flat = qq[:].rearrange("p s w d -> p (s w d)")
                    for h in range(Q_HEADS):
                        for j in range(ST):
                            at = h * S + j * P
                            last = pe.transpose(flat[:, at:at + P],
                                                f32(q_rows[:, j, h]).rearrange("p w d -> p (w d)"), t["ident"][:])
                    last.then_inc(s["q_turned"], 1)
                if att:
                    turn_weights(b, 3)
                    head_values(b, 3, r)

            steps(pe, step)


def ffn1_front(nc, sem, t, a):
    with ExitStack() as ctx:
        def tile(name, shape, dt=F32):
            return ctx.enter_context(nc.sbuf_tensor(name, shape, dt))

        def bank(name, shape):
            return ctx.enter_context(nc.psum_tensor(name, shape, F32))

        gate_raw = tile("h_gate_raw", [P, KC, P])
        gate_hi = tile("h_gate_hi", [P, KC, P], F32R)
        gate_lo = tile("h_gate_lo", [P, KC, P], F32R)
        rows = tile("h_rows", [P, 2, TPC, D])
        stats = tile("h_stats", [P, NT, 6])
        mean_var = tile("h_mean_var", [P, NT, 2])
        std = tile("h_std", [P, NT])
        rstd = tile("h_rstd", [P, NT])
        logitsT = tile("h_logitsT", [EXPERTS, TOK])
        turned = bank("h_turned", [P, 2, KC, CH])
        logits = bank("h_logits", [P, KC, CH])

        loaded = sem("h_loaded")
        w_split = sem("h_w_split")
        stats_step = sem("h_stats_step")
        stats_done = sem("h_stats_done")
        std_done = sem("h_std_done")
        rstd_done = sem("h_rstd_done")
        normed = sem("h_normed")
        x_turned = sem("h_x_turned")
        x_hi = sem("h_x_hi")
        x_lo = sem("h_x_lo")
        logits_ready = sem("h_logits_ready")
        logits_out = sem("h_logits_out")
        logits_turned = sem("h_logits_turned")
        logits_rows = sem("h_logits_rows")

        block = ctx.enter_context(nc.Block())

        @block.sync
        def _(sp):
            sp.dma_start(gate_raw[:], a["gate1"].rearrange("(k p) n -> p k n", p=P)).then_inc(loaded, 16)
            sp.dma_start(t["before"][:], a["before"].partition_broadcast(P)).then_inc(loaded, 16)
            for e in range(2):
                sp.dma_start(t["e_raw"][:, e], a["experts1"][e].rearrange("m (k p) n -> p (m k) n", p=P))\
                    .then_inc(t["e_loaded"][e], 16)
            sp.wait_ge(loaded, 32)

        @block.gpsimd
        def _(pool):
            pool.wait_ge(loaded, 32)
            split_weights(pool, gate_raw[:], gate_hi[:], gate_lo[:], w_split, 0)
            for e in range(2):
                pool.wait_ge(t["e_loaded"][e], 16)
                split_weights(pool, t["e_raw"][:, e], t["e_hi"][:, e], t["e_lo"][:, e], t["e_split"], 2 * e)

        @block.scalar
        def _(act):
            act.wait_ge(stats_done, NT)
            act.activation(std[:], mean_var[:, :, 1], ACT.Sqrt, bias=t["ln_eps"][:]).then_inc(std_done, 1)
            for c in range(NCH):
                act.wait_ge(x_turned, c + 1)
                act.activation(t["hT_hi"][:, :, bass.ts(c, CH)], turned[:, c % 2], ACT.Copy).then_inc(x_hi, 1)
            for c in range(NCH):
                act.wait_ge(logits_ready, c + 1)
                act.activation(logitsT[:, bass.ts(c, CH)], logits[0:EXPERTS, c % KC, :], ACT.Copy)\
                    .then_inc(logits_out, 1)
            act.wait_ge(logits_turned, 1)
            act.activation(t["logits"][:], turned[:, 0, 0, 0:NT * EXPERTS].rearrange("p (n e) -> p n e", e=EXPERTS),
                           ACT.Copy).then_inc(logits_rows, 1)

        @block.vector
        def _(dve):
            for j in range(NT):
                dve.bn_stats(stats[:, j, :], t["x_res"][:, j, :]).then_inc(stats_step, 1)
            for j in range(NT):
                dve.wait_ge(stats_step, j + 1)
                dve.bn_aggr(mean_var[:, j, :], stats[:, j, :]).then_inc(stats_done, 1)
            dve.wait_ge(std_done, 1)
            dve.reciprocal(rstd[:], std[:]).then_inc(rstd_done, 1)
            dve.wait_ge(rstd_done, 1)
            for c in range(NCH + 1):
                if c < NCH:
                    if c >= 2:
                        dve.wait_ge(x_turned, c - 1)
                    normalise_chunk(dve, rows[:, c % 2], t["x_res"], rstd, mean_var, c, None, normed)
                if c >= 1:
                    dve.wait_ge(x_hi, c)
                    dve.tensor_tensor(t["hT_lo"][:, :, bass.ts(c - 1, CH)], turned[:, (c - 1) % 2],
                                      f32(t["hT_hi"][:, :, bass.ts(c - 1, CH)]), ALU.subtract).then_inc(x_lo, 1)

        @block.tensor
        def _(pe):
            for c in range(NCH + 1):
                if c < NCH:
                    pe.wait_ge(normed, c + 1)
                    if c >= 2:
                        pe.wait_ge(x_lo, c - 1)
                    turn_chunk(pe, turned[:, c % 2], rows[:, c % 2], t["ident"][:]).then_inc(x_turned, 1)
                if c >= 1:
                    n = c - 1
                    pe.wait_ge(w_split, 2)
                    pe.wait_ge(x_lo, n + 1)
                    if n >= KC:
                        pe.wait_ge(logits_out, n - KC + 1)
                    for kc in range(KC):
                        last = split_products(pe, logits[:, n % KC, :], (gate_hi[:, kc, :], gate_lo[:, kc, :]),
                                              (t["hT_hi"][:, kc, bass.ts(n, CH)], t["hT_lo"][:, kc, bass.ts(n, CH)]),
                                              kc == 0, kc == KC - 1)
                    last.then_inc(logits_ready, 1)
            pe.wait_ge(logits_out, NCH)
            for n in range(NT):
                last = pe.transpose(turned[:, 0, 0, bass.ts(n, EXPERTS)], logitsT[:, bass.ts(n, P)],
                                    t["ident"][0:EXPERTS, 0:EXPERTS])
            last.then_inc(logits_turned, 1)


def build_program(nc, a, out):
    with ExitStack() as ctx:
        def tile(name, shape, dt=F32):
            return ctx.enter_context(nc.sbuf_tensor(name, shape, dt))

        phase_sems = []

        def sem(name):
            phase_sems.append(nc.alloc_semaphore(name=name))
            return phase_sems[-1]

        def next_phase():
            nc.clear_and_free_semaphores(phase_sems)
            phase_sems.clear()
            nc.all_engine_barrier()

        t = {name: tile(name, shape) for name, shape in (
            ("ident", [P, P]), ("x_res", [P, NT, D]), ("ln_eps", [P, 1]))}
        t["passed"] = ctx.enter_context(nc.semaphore("passed"))
        t["ident_r"] = tile("ident_r", [P, P], F32R)
        with ExitStack() as first:
            def part(name, shape, dt=F32):
                t[name] = first.enter_context(nc.sbuf_tensor(name, shape, dt))
            part("head_rows", [P, P // HD])
            for name in ("qT_hi", "qT_lo", "kT_hi", "kT_lo"):
                part(name, [P, KC, TOK], F32R)
            part("v_all", [P, NT, D])
            part("mask_bias", [P, NT, S], F32R)
            for name in ("all_masked", "scale", "neg_scale", "mask_depth"):
                part(name, [P, NT])
            part("o_bias", [P, D])
            part("wo_hi", [P, KC, D], F32R)
            part("wo_lo", [P, KC, D], F32R)
            with ExitStack() as raw:
                t["wo_raw"] = raw.enter_context(nc.sbuf_tensor("wo_raw", [P, KC, D], F32))
                attention0_projections(nc, sem, t, a)
            attention0(nc, sem, t, a)
        next_phase()
        with ExitStack() as second:
            def part(name, shape, dt=F32):
                t[name] = second.enter_context(nc.sbuf_tensor(name, shape, dt))
            part("hT_hi", [P, KC, TOK], F32R)
            part("hT_lo", [P, KC, TOK], F32R)
            part("mixed", [P, NT, D])
            part("logits", [P, NT, EXPERTS])
            part("combine", [P, NT, HALVES])
            part("before", [P, EXPERTS * EXPERTS])
            part("e_raw", [P, 2, 3 * KC, D])
            part("e_hi", [P, 2, 3 * KC, D], F32R)
            part("e_lo", [P, 2, 3 * KC, D], F32R)
            t["e_loaded"] = [sem(f"e_loaded{n}") for n in range(2)]
            t["e_split"] = sem("e_split")
            t["ones_set"] = sem("ones_set")
            ffn0_front(nc, sem, t, a)
            mixture(nc, sem, t, a["experts0"], HALVES, 1, 4)
            ffn0_back(nc, sem, t, a)
        next_phase()
        attention1(nc, sem, t, a)
        next_phase()
        with ExitStack() as fourth:
            def part(name, shape, dt=F32):
                t[name] = fourth.enter_context(nc.sbuf_tensor("l1_" + name, shape, dt))
            part("hT_hi", [P, KC, TOK], F32R)
            part("hT_lo", [P, KC, TOK], F32R)
            t["mixed"] = t["x_res"]
            part("logits", [P, NT, EXPERTS])
            part("combine", [P, NT, 3 * EXPERTS])
            part("before", [P, EXPERTS * EXPERTS])
            part("e_raw", [P, 2, 3 * KC, D])
            part("e_hi", [P, 2, 3 * KC, D], F32R)
            part("e_lo", [P, 2, 3 * KC, D], F32R)
            t["e_loaded"] = [sem(f"l1_e_loaded{n}") for n in range(2)]
            t["e_split"] = sem("l1_e_split")
            t["ones_set"] = None
            ffn1_front(nc, sem, t, a)
            mixture(nc, sem, t, a["experts1"], 3 * EXPERTS, 3, 2)
        stored = sem("out_stored")
        block = ctx.enter_context(nc.Block())

        @block.sync
        def _(sp):
            sp.dma_start(out.rearrange("(j p) d -> p j d", p=P), t["x_res"][:]).then_inc(stored, 16)
            sp.wait_ge(stored, 16)


def _columns(np, *vectors):
    return np.stack([v.reshape(KC, P) for v in vectors]).transpose(2, 0, 1)


def _swap_halves(np, w):
    return w.reshape(D, -1, 2, Q_HD // 2)[:, :, ::-1].reshape(D, -1)


def _thirds(np, w):
    padded = np.zeros((EXPERTS, D, 3 * D), np.float32)
    padded[:, :, :w.shape[2]] = w
    return padded.reshape(EXPERTS, D, 3, D).transpose(0, 2, 1, 3)


def _rope_tables(np):
    f = np.float32
    timescale = f(10000.0) ** (f(2.0 / Q_HD) * np.arange(Q_HD // 2, dtype=f))
    tables = []
    for start in (S, 0):
        radians = (np.arange(start, start + S).astype(f)[:, None] / timescale).astype(f)
        cos, sin = np.cos(radians).astype(f), np.sin(radians).astype(f)
        tables += [np.concatenate([cos, cos], 1), np.concatenate([-sin, sin], 1)]
    return np.stack(tables).reshape(4, ST, P, Q_HD).transpose(2, 0, 1, 3)


def _lay_out(np, i):
    def l0(name):
        return i["L0_ffn_" + name]

    ins = dict(x=i["x"].reshape(TOK, D), ctx=i["ctx_1024"].reshape(TOK, D),
               mask0=i["mask_Bx1xSxS2_ik1"].reshape(TOK, S), ident=np.eye(P, dtype=np.float32))
    ins["head_rows"] = np.kron(np.eye(P // HD, dtype=np.float32), np.ones((HD, 1), np.float32))
    for n in "QKVO":
        ins["w" + n] = i[f"L0_xattn_w{n}_w"].T
        ins["b" + n] = i[f"L0_xattn_w{n}_b"]
    for n in ("bQ", "bK"):
        ins[n] = ins[n].reshape(KC, P).T
    ins["col_bias0"] = _columns(np, l0("lin0_b"), l0("swi1_b1"), l0("swi1_b2"))
    ins["col_bias1"] = l0("lin1_b").reshape(KC, P).T
    for n in ("lin0_w", "swi1_w1", "swi1_w2", "lin1_w", "swi2_w1", "swi2_w2", "swi2_b1", "swi2_b2"):
        ins[n] = l0(n)
    for n, w in (("gate0", l0("gate_w")), ("gate1", i["L1_ffn_w_router"])):
        ins[n] = np.zeros((D, P), np.float32)
        ins[n][:, :EXPERTS] = w.T
    ins["before"] = np.tril(np.ones((EXPERTS, EXPERTS), np.float32), -1).reshape(-1)
    shared = [np.stack([l0("sh_w1")[:, h:h + D], l0("sh_w3")[:, h:h + D], l0("sh_w2")[h:h + D]]) for h in (0, D)]
    ins["experts0"] = np.concatenate([np.stack([l0("exp_w1"), l0("exp_w3"), l0("exp_w2")], 1), np.stack(shared)])
    q = i["L1_xattn_q_w"].transpose(1, 0, 2).reshape(D, D)
    k, v = i["L1_xattn_kv_w"][:, 0]
    ins["wq1"] = np.concatenate([q, _swap_halves(np, q)], 1)
    ins["wkv1"] = np.concatenate([k, _swap_halves(np, k), v, v], 1)
    ins["wo1"] = i["L1_xattn_out_w"].reshape(D, D)
    ins["rms_gain"] = i["L1_xattn_rms_scale"].reshape(KC, P).T
    ins["mask1"] = np.ascontiguousarray(i["mask_BxS2_bk0"]).reshape(-1).view(np.int32)
    ins["rope"] = _rope_tables(np)
    gate, up = (_thirds(np, i["L1_ffn_" + n].transpose(0, 2, 1)) for n in ("w_gate", "w_up"))
    down = _thirds(np, i["L1_ffn_w_down"]).transpose(0, 1, 3, 2)
    ins["experts1"] = np.stack([gate, up, down], 2).reshape(3 * EXPERTS, 3, D, D)
    return ins


def kernel(**inputs):
    import numpy as np
    import concourse.bacc as bacc
    from concourse.bass_utils import run_bass_kernel_spmd as run

    nc = bacc.Bacc("TRN2", target_bir_lowering=False, num_devices=1)
    arrays, args = {}, {}
    for name, a in _lay_out(np, {n: np.asarray(a) for n, a in inputs.items()}).items():
        a = np.ascontiguousarray(a)
        arrays[f"in_{name}_dram"] = a
        args[name] = nc.dram_tensor(f"in_{name}_dram", a.shape, mybir.dt.from_np(a.dtype), kind="ExternalInput").ap()
    out = nc.dram_tensor("out_0_dram", (TOK, D), F32, kind="ExternalOutput").ap()
    build_program(nc, args, out)
    r = run(nc, [arrays], core_ids=[0])
    return r.results[0]["out_0_dram"].reshape(B, S, D)
```
